# Optimizing a Trainium2 kernel written in Bass

```python
import numpy as np
import jax
import jax.numpy as jnp

def _softmax(x, axis=-1):
    return jax.nn.softmax(x, axis=axis)

def _gelu(x):
    return jax.nn.gelu(x, approximate=True)

def _silu(x):
    return jax.nn.silu(x)

def _sigmoid(x):
    return jax.nn.sigmoid(x)

def _layernorm(x, axis=-1, eps=1e-05):
    m = jnp.mean(x, axis=axis, keepdims=True)
    v = jnp.var(x, axis=axis, keepdims=True)
    return (x - m) / jnp.sqrt(v + eps)

def _scatter_add(tgt, idx, src, axis=0):
    return tgt.at[idx].add(src)

def _segment_sum(src, seg, n):
    return jax.ops.segment_sum(src, seg, n)
kernel_name = 'mk_audio_tower_d1_tok_aud1d1024_r4_0ade34'

def setup_inputs(seed: int=0):
    np.random.seed(seed)
    _w = jnp.asarray

    def _rec_inputs():
        import jax
        import jax.numpy as jnp
        _rk = jax.random.key(seed)
        x = -9.80646e-05 + 1.00041 * jax.random.normal(jax.random.fold_in(_rk, 1), (64, 4000), jnp.float32)
        return x
    x = _rec_inputs()

    def _L0_tok_setup():
        import jax, jax.numpy as jnp
        import numpy as np
        D_MODEL = 256
        PATCH_LEN = 32
        D_K = D_MODEL // 4
        N_HEADS = 4

        def _pos_encoding(seq_len, d_model):
            pos = jnp.arange(seq_len, dtype=jnp.float32)[:, None]
            div = jnp.exp(jnp.arange(0, d_model, 2, dtype=jnp.float32) * (-np.log(10000.0) / d_model))
            ang = pos * div
            return jnp.stack([jnp.sin(ang), jnp.cos(ang)], axis=-1).reshape(seq_len, d_model)
        key = jax.random.key(seed)
        ks = jax.random.split(key, 24)
        B, L = (16, 8192)

        def n(k, shape, scale=0.02):
            return jax.random.normal(k, shape, dtype=jnp.float32) * scale
        return {'X': jax.random.normal(ks[0], (B, L), dtype=jnp.float32), 'Wp': n(ks[1], (D_MODEL, PATCH_LEN)), 'bp': n(ks[2], (D_MODEL,)), 'rb1_hw': n(ks[3], (128, D_MODEL)), 'rb1_hb': n(ks[4], (128,)), 'rb1_fw': n(ks[5], (D_MODEL, 128)), 'rb1_fb': n(ks[6], (D_MODEL,)), 'Wq': n(ks[7], (N_HEADS, D_K, D_MODEL)), 'bq': n(ks[8], (N_HEADS, D_K)), 'Wk': n(ks[9], (N_HEADS, D_K, D_MODEL)), 'bk': n(ks[10], (N_HEADS, D_K)), 'Wv': n(ks[11], (N_HEADS, D_K, D_MODEL)), 'bv': n(ks[12], (N_HEADS, D_K)), 'f1w': n(ks[13], (4 * D_MODEL, D_MODEL)), 'f1b': n(ks[14], (4 * D_MODEL,)), 'f2w': n(ks[15], (D_MODEL, 4 * D_MODEL)), 'f2b': n(ks[16], (D_MODEL,)), 'rb2_hw': n(ks[17], (128, D_MODEL)), 'rb2_hb': n(ks[18], (128,)), 'rb2_fw': n(ks[19], (D_MODEL, 128)), 'rb2_fb': n(ks[20], (D_MODEL,))}
    _L0_tok_all = _L0_tok_setup()
    _L0_tok_in = {k: v for k, v in _L0_tok_all.items() if k in ('Wp', 'bp', 'rb1_hw', 'rb1_hb', 'rb1_fw', 'rb1_fb', 'Wq', 'bq', 'Wk', 'bk', 'Wv', 'bv', 'f1w', 'f1b', 'f2w', 'f2b', 'rb2_hw', 'rb2_hb', 'rb2_fw', 'rb2_fb')}
    del _L0_tok_all

    def _L0_attn_setup():
        import jax, jax.numpy as jnp
        import numpy as np
        D_MODEL = 256
        D_STATE = 16
        EXPAND = 2
        D_INNER = D_MODEL * EXPAND
        DT_RANK = (D_MODEL + 15) // 16
        BATCH = 2
        SEQ = 256

        def _s6_forward(x, W_in, W_conv, W_x, W_dt, b_dt, A_log, D_param, W_out):
            B, L, _ = x.shape
            u, res = jnp.split(x @ W_in, 2, axis=-1)
            up = jnp.pad(u, ((0, 0), (2, 0), (0, 0)))
            u = up[:, :L] * W_conv[:, 0] + up[:, 1:L + 1] * W_conv[:, 1] + up[:, 2:L + 2] * W_conv[:, 2]
            u = jax.nn.silu(u)
            x_dbl = u @ W_x
            dt, Bm, Cm = jnp.split(x_dbl, [DT_RANK, DT_RANK + D_STATE], axis=-1)
            delta = jax.nn.softplus(dt @ W_dt + b_dt)
            A = -jnp.exp(A_log)
            deltaA = jnp.exp(jnp.einsum('bld,dn->bldn', delta, A))
            deltaB_u = jnp.einsum('bld,bln->bldn', delta * u, Bm)

            def step(h, inp):
                dA, dbu, c = inp
                h = dA * h + dbu
                y = jnp.einsum('bdn,bn->bd', h, c)
                return (h, y)
            h0 = jnp.zeros((B, D_INNER, D_STATE), dtype=u.dtype)
            _, ys = jax.lax.scan(step, h0, (jnp.moveaxis(deltaA, 1, 0), jnp.moveaxis(deltaB_u, 1, 0), jnp.moveaxis(Cm, 1, 0)))
            y = jnp.moveaxis(ys, 0, 1)
            y = y + u * D_param
            y = y * jax.nn.silu(res)
            return y @ W_out
        key = jax.random.key(seed)
        ks = jax.random.split(key, 8)

        def nrm(k, shape, scale):
            return jax.random.normal(k, shape, dtype=jnp.float32) * scale
        x = jax.random.normal(ks[0], (BATCH, SEQ, D_MODEL), dtype=jnp.float32)
        W_in = nrm(ks[1], (D_MODEL, 2 * D_INNER), D_MODEL ** (-0.5))
        W_conv = nrm(ks[2], (D_INNER, 3), 3 ** (-0.5))
        W_x = nrm(ks[3], (D_INNER, DT_RANK + 2 * D_STATE), D_INNER ** (-0.5))
        W_dt = nrm(ks[4], (DT_RANK, D_INNER), DT_RANK ** (-0.5))
        b_dt = nrm(ks[5], (D_INNER,), 0.1)
        A_log = jnp.log(jnp.tile(jnp.arange(1, D_STATE + 1, dtype=jnp.float32), (D_INNER, 1)))
        D_param = jnp.ones((D_INNER,), dtype=jnp.float32)
        W_out = nrm(ks[6], (D_INNER, D_MODEL), D_INNER ** (-0.5))
        return {'x': x, 'W_in': W_in, 'W_conv': W_conv, 'W_x': W_x, 'W_dt': W_dt, 'b_dt': b_dt, 'A_log': A_log, 'D_param': D_param, 'W_out': W_out}
    _L0_attn_all = _L0_attn_setup()
    _L0_attn_in = {k: v for k, v in _L0_attn_all.items() if k in ('W_in', 'W_conv', 'W_x', 'W_dt', 'b_dt', 'A_log', 'D_param', 'W_out')}
    del _L0_attn_all

    def _L0_ffn_setup():
        import jax, jax.numpy as jnp
        import numpy as np
        EPS = 1e-08

        def _ternary_linear(x, w):
            alpha = jnp.mean(jnp.abs(w))
            w_t = jnp.sign(w) * (jnp.abs(w) > 0.5 * alpha).astype(w.dtype)
            w_q = w + jax.lax.stop_gradient(w_t - w)
            d = x.shape[-1]
            rms = jnp.sqrt(jnp.sum(x * x, axis=-1, keepdims=True)) / jnp.sqrt(jnp.asarray(d, x.dtype))
            x_norm = x / (rms + EPS)
            return jnp.einsum('bsd,fd->bsf', x_norm, w_q)
        key = jax.random.key(seed)
        k1, k2, k3 = jax.random.split(key, 3)
        d_model, d_ff = (256, 1024)
        B, S = (4, 1024)
        x = jax.random.normal(k1, (B, S, d_model), dtype=jnp.float32)
        w_up = jax.random.normal(k2, (d_ff, d_model), dtype=jnp.float32) * 0.02
        w_down = jax.random.normal(k3, (d_model, d_ff), dtype=jnp.float32) * 0.02
        return {'x': x, 'w_up': w_up, 'w_down': w_down}
    _L0_ffn_all = _L0_ffn_setup()
    _L0_ffn_in = {k: v for k, v in _L0_ffn_all.items() if k in ('w_up', 'w_down')}
    del _L0_ffn_all
    return {'x': x, 'L0_tok_Wp': _L0_tok_in['Wp'], 'L0_tok_bp': _L0_tok_in['bp'], 'L0_tok_rb1_hw': _L0_tok_in['rb1_hw'], 'L0_tok_rb1_hb': _L0_tok_in['rb1_hb'], 'L0_tok_rb1_fw': _L0_tok_in['rb1_fw'], 'L0_tok_rb1_fb': _L0_tok_in['rb1_fb'], 'L0_tok_Wq': _L0_tok_in['Wq'], 'L0_tok_bq': _L0_tok_in['bq'], 'L0_tok_Wk': _L0_tok_in['Wk'], 'L0_tok_bk': _L0_tok_in['bk'], 'L0_tok_Wv': _L0_tok_in['Wv'], 'L0_tok_bv': _L0_tok_in['bv'], 'L0_tok_f1w': _L0_tok_in['f1w'], 'L0_tok_f1b': _L0_tok_in['f1b'], 'L0_tok_f2w': _L0_tok_in['f2w'], 'L0_tok_f2b': _L0_tok_in['f2b'], 'L0_tok_rb2_hw': _L0_tok_in['rb2_hw'], 'L0_tok_rb2_hb': _L0_tok_in['rb2_hb'], 'L0_tok_rb2_fw': _L0_tok_in['rb2_fw'], 'L0_tok_rb2_fb': _L0_tok_in['rb2_fb'], 'L0_attn_W_in': _L0_attn_in['W_in'], 'L0_attn_W_conv': _L0_attn_in['W_conv'], 'L0_attn_W_x': _L0_attn_in['W_x'], 'L0_attn_W_dt': _L0_attn_in['W_dt'], 'L0_attn_b_dt': _L0_attn_in['b_dt'], 'L0_attn_A_log': _L0_attn_in['A_log'], 'L0_attn_D_param': _L0_attn_in['D_param'], 'L0_attn_W_out': _L0_attn_in['W_out'], 'L0_ffn_w_up': _L0_ffn_in['w_up'], 'L0_ffn_w_down': _L0_ffn_in['w_down']}

def reference(x, L0_tok_Wp, L0_tok_bp, L0_tok_rb1_hw, L0_tok_rb1_hb, L0_tok_rb1_fw, L0_tok_rb1_fb, L0_tok_Wq, L0_tok_bq, L0_tok_Wk, L0_tok_bk, L0_tok_Wv, L0_tok_bv, L0_tok_f1w, L0_tok_f1b, L0_tok_f2w, L0_tok_f2b, L0_tok_rb2_hw, L0_tok_rb2_hb, L0_tok_rb2_fw, L0_tok_rb2_fb, L0_attn_W_in, L0_attn_W_conv, L0_attn_W_x, L0_attn_W_dt, L0_attn_b_dt, L0_attn_A_log, L0_attn_D_param, L0_attn_W_out, L0_ffn_w_up, L0_ffn_w_down):
    import jax
    import jax.numpy as jnp

    def _L0_tok_ref(X, Wp, bp, rb1_hw, rb1_hb, rb1_fw, rb1_fb, Wq, bq, Wk, bk, Wv, bv, f1w, f1b, f2w, f2b, rb2_hw, rb2_hb, rb2_fw, rb2_fb):
        import jax, jax.numpy as jnp
        import numpy as np
        D_MODEL = 256
        PATCH_LEN = 32
        D_K = D_MODEL // 4
        N_HEADS = 4

        def _pos_encoding(seq_len, d_model):
            pos = jnp.arange(seq_len, dtype=jnp.float32)[:, None]
            div = jnp.exp(jnp.arange(0, d_model, 2, dtype=jnp.float32) * (-np.log(10000.0) / d_model))
            ang = pos * div
            return jnp.stack([jnp.sin(ang), jnp.cos(ang)], axis=-1).reshape(seq_len, d_model)
        B, L = X.shape
        S = L // PATCH_LEN
        x = X.reshape(B, S, PATCH_LEN) @ Wp.T + bp
        x = x + _pos_encoding(S, D_MODEL)[None]
        x = (x @ rb1_hw.T + rb1_hb) @ rb1_fw.T + rb1_fb + x
        q = jnp.einsum('bsd,hkd->bhsk', x, Wq) + bq[None, :, None, :]
        k = jnp.einsum('bsd,hkd->bhsk', x, Wk) + bk[None, :, None, :]
        v = jnp.einsum('bsd,hkd->bhsk', x, Wv) + bv[None, :, None, :]
        scores = jnp.einsum('bhsk,bhtk->bhst', q, k) / jnp.sqrt(jnp.float32(D_K))
        attn = jax.nn.softmax(scores, axis=-1)
        o = jnp.einsum('bhst,bhtk->bhsk', attn, v)
        x = o.transpose(0, 2, 1, 3).reshape(B, S, D_MODEL)
        x = jax.nn.relu(x @ f1w.T + f1b) @ f2w.T + f2b
        x = (x @ rb2_hw.T + rb2_hb) @ rb2_fw.T + rb2_fb + x
        return x

    def _L0_attn_ref(x, W_in, W_conv, W_x, W_dt, b_dt, A_log, D_param, W_out):
        import jax, jax.numpy as jnp
        import numpy as np
        D_MODEL = 256
        D_STATE = 16
        EXPAND = 2
        D_INNER = D_MODEL * EXPAND
        DT_RANK = (D_MODEL + 15) // 16
        BATCH = 2
        SEQ = 256

        def _s6_forward(x, W_in, W_conv, W_x, W_dt, b_dt, A_log, D_param, W_out):
            B, L, _ = x.shape
            u, res = jnp.split(x @ W_in, 2, axis=-1)
            up = jnp.pad(u, ((0, 0), (2, 0), (0, 0)))
            u = up[:, :L] * W_conv[:, 0] + up[:, 1:L + 1] * W_conv[:, 1] + up[:, 2:L + 2] * W_conv[:, 2]
            u = jax.nn.silu(u)
            x_dbl = u @ W_x
            dt, Bm, Cm = jnp.split(x_dbl, [DT_RANK, DT_RANK + D_STATE], axis=-1)
            delta = jax.nn.softplus(dt @ W_dt + b_dt)
            A = -jnp.exp(A_log)
            deltaA = jnp.exp(jnp.einsum('bld,dn->bldn', delta, A))
            deltaB_u = jnp.einsum('bld,bln->bldn', delta * u, Bm)

            def step(h, inp):
                dA, dbu, c = inp
                h = dA * h + dbu
                y = jnp.einsum('bdn,bn->bd', h, c)
                return (h, y)
            h0 = jnp.zeros((B, D_INNER, D_STATE), dtype=u.dtype)
            _, ys = jax.lax.scan(step, h0, (jnp.moveaxis(deltaA, 1, 0), jnp.moveaxis(deltaB_u, 1, 0), jnp.moveaxis(Cm, 1, 0)))
            y = jnp.moveaxis(ys, 0, 1)
            y = y + u * D_param
            y = y * jax.nn.silu(res)
            return y @ W_out
        return _s6_forward(x, W_in, W_conv, W_x, W_dt, b_dt, A_log, D_param, W_out)

    def _L0_ffn_ref(x, w_up, w_down):
        import jax, jax.numpy as jnp
        import numpy as np
        EPS = 1e-08

        def _ternary_linear(x, w):
            alpha = jnp.mean(jnp.abs(w))
            w_t = jnp.sign(w) * (jnp.abs(w) > 0.5 * alpha).astype(w.dtype)
            w_q = w + jax.lax.stop_gradient(w_t - w)
            d = x.shape[-1]
            rms = jnp.sqrt(jnp.sum(x * x, axis=-1, keepdims=True)) / jnp.sqrt(jnp.asarray(d, x.dtype))
            x_norm = x / (rms + EPS)
            return jnp.einsum('bsd,fd->bsf', x_norm, w_q)
        h = jax.nn.gelu(_ternary_linear(x, w_up), approximate=False)
        return _ternary_linear(h, w_down)
    h = _L0_tok_ref(x, L0_tok_Wp, L0_tok_bp, L0_tok_rb1_hw, L0_tok_rb1_hb, L0_tok_rb1_fw, L0_tok_rb1_fb, L0_tok_Wq, L0_tok_bq, L0_tok_Wk, L0_tok_bk, L0_tok_Wv, L0_tok_bv, L0_tok_f1w, L0_tok_f1b, L0_tok_f2w, L0_tok_f2b, L0_tok_rb2_hw, L0_tok_rb2_hb, L0_tok_rb2_fw, L0_tok_rb2_fb)
    h = h + _L0_attn_ref(_layernorm(h, axis=-1), L0_attn_W_in, L0_attn_W_conv, L0_attn_W_x, L0_attn_W_dt, L0_attn_b_dt, L0_attn_A_log, L0_attn_D_param, L0_attn_W_out)
    h = h + _L0_ffn_ref(_layernorm(h, axis=-1), L0_ffn_w_up, L0_ffn_w_down)
    return h

_drawn_inputs = setup_inputs


def setup_inputs(seed=0):
    import zlib

    import numpy as np

    out = dict(_drawn_inputs(seed))
    spreads = {'L0_attn_D_param': (1.0, 0.2)}
    factors = {'x': 3.148,
     'L0_tok_Wp': 3.065,
     'L0_tok_rb1_hb': 5.061,
     'L0_tok_Wq': 7.471,
     'L0_tok_bq': 8.0,
     'L0_tok_Wk': 5.657,
     'L0_tok_bk': 8.0,
     'L0_attn_b_dt': 2.95}
    for name, (base, spread) in spreads.items():
        noise = np.random.default_rng([zlib.crc32(name.encode()), seed]).standard_normal(out[name].shape)
        drawn = base * np.exp(spread * noise) if base else spread * noise
        out[name] = jnp.asarray(drawn.astype(out[name].dtype))
    for name, factor in factors.items():
        out[name] = (out[name] * factor).astype(out[name].dtype)
    return out
```

```python
from contextlib import ExitStack

import numpy as np

import concourse.bass as bass
from concourse import mybir

F32 = mybir.dt.float32
F16 = mybir.dt.float16
ALU = mybir.AluOpType
ACT = mybir.ActivationFunctionType
AX = mybir.AxisListType

P = 128
B, S, PATCH, D = 64, 125, 32, 256
HEADS, DK = 4, 64
FF = 1024
DI, NS, DT_RANK = 512, 16, 16
NB = 4
T = NB * S
GROUPS = B // NB
KD, KI, KF = D // P, DI // P, FF // P
Z = PATCH + S
LN_EPS, RMS_EPS = 1e-5, 1e-8
SLOTS = 4
UNITS = 2 * NS
HT = KI // 2
DA_SLOTS, W_SLOTS, BC_SLOTS = 3, 5, 2
PAIRS = NS // 2

POST = [("z", 4, None), ("w_out", 2, "dve"), ("norm2", 1, None), ("turn2", KD, "dve"), ("up", KF, "act"),
        ("sumsq", 1, "dve"), ("down", 2, "dve")]
PRE = ([("qk", 4, "dve"), ("v", 2, "dve")]
       + [(n, 1, f) for i in range(2) for n, f in
          [("score", "act"), ("score", "act"), ("turn_p", "act"), ("turn_p", "act"), ("pv", "act")]]
       + [("f1", KF, "act"), ("f2", 2, "dve"), ("norm1", 1, None), ("turn1", KD, "act"),
          ("w_in", 2 * KI, "act"), ("silu", KI, None), ("w_x", 1, "act"), ("w_dt", KI, "dve"),
          ("delta", 1, None)])
COST = dict(z=0.6, w_out=4, norm2=2, turn2=1, up=1.2, sumsq=1.7, down=4.5, qk=0.9, v=1, score=2, turn_p=1, pv=2,
            f1=1.8, f2=8, norm1=2, turn1=1, w_in=1.8, silu=0.5, w_x=3.6, w_dt=0.9, delta=4)


def schedule(post, pre):
    seen, order = {}, []
    for name, n, freed_by in (POST if post else []) + (PRE if pre else []):
        for _ in range(n):
            i = seen[name] = seen.get(name, -1) + 1
            order.append((name, i, freed_by))
    total = sum(COST[name] for name, _, _ in order)
    at, tile, freed, t, c = {j: [] for j in range(UNITS)}, {}, {}, 0, 0.0
    count = {"act": 0, "dve": 0}
    frees = []
    for name, i, freed_by in order:
        at[min(UNITS - 1, int(c / total * UNITS))].append((name, i))
        c += COST[name]
        if freed_by:
            count[freed_by] += 1
            tile[name, i] = t
            freed[name, i] = (freed_by, count[freed_by])
            frees.append((freed_by, count[freed_by]))
            t += 1
    return at, tile, freed, frees


def build(nc, ins, out):
    with ExitStack() as ctx:
        def sb(name, shape, dt=F32):
            return ctx.enter_context(nc.sbuf_tensor(name, shape, dt))

        sems = []

        def sem(name):
            s = ctx.enter_context(nc.semaphore(name))
            sems.append(s)
            return s

        ident = sb("ident", [P, P])
        ones = sb("ones", [P, P])
        w_qk = sb("w_qk", [PATCH, 2 * D])
        w_v = sb("w_v", [PATCH, D])
        pos_qk = sb("pos_qk", [P, 4, S])
        pos_v = sb("pos_v", [S, D])
        w_f1 = sb("w_f1", [P, KD, FF])
        b_f1 = sb("b_f1", [P, KF])
        w_f2 = sb("w_f2", [P, KF, D])
        b_f2 = sb("b_f2", [S, D])
        w_in = sb("w_in", [P, KD, 2 * DI])
        w_conv = sb("w_conv", [P, KI, 3])
        w_x = sb("w_x", [P, KI, DT_RANK + 2 * NS])
        w_dt = sb("w_dt", [DT_RANK, DI])
        b_dt = sb("b_dt", [P, KI])
        neg_a = sb("neg_a", [P, KI, NS])
        d_col = sb("d_col", [P, KI])
        d_diag = sb("d_diag", [P, KI, P])
        w_out = sb("w_out", [P, KI, D])
        w_up = sb("w_up", [P, KD, FF], F16)
        w_down = sb("w_down", [P, KF, D], F16)
        half = sb("half", [S, 2 * NB])
        minus_half = sb("minus_half", [S, NB])

        patches = sb("patches", [PATCH, T])
        region_a = sb("region_a", [P, NB * D + KD * T])
        region_b = sb("region_b", [P, KF * T])
        qk = region_a[:, 0:4 * T].rearrange("p (m t) -> p m t", m=4)
        gated = qk
        xn = region_a[0:S, 0:NB * D].rearrange("p (b d) -> p b d", b=NB)
        xn_t = region_a[:, NB * D:NB * D + KD * T].rearrange("p (k t) -> p k t", k=KD)
        xn_parts = region_a[:, NB * D:NB * D + KD * T].bitcast(F16).rearrange("p (c k t) -> p c k t", c=2, k=KD)
        relu = region_b[:, :].rearrange("p (m t) -> p m t", m=KF)
        g_parts = region_b[:, :].bitcast(F16).rearrange("p (c m t) -> p c m t", c=2, m=KF)
        v_tok = region_b[0:S, 0:NB * D].rearrange("p (b d) -> p b d", b=NB)
        probs = region_b[0:S, 1024:1024 + 2 * T].rearrange("p (i c t) -> p i c t", i=2, c=4)
        probs_t = region_b[0:S, 1024 + 2 * T:1024 + 4 * T].rearrange("p (i c t) -> p i c t", i=2, c=4)
        padded = region_b[:, 0:KI * NB * (S + 2)].rearrange("p (m b t) -> p m b t", m=KI, b=NB)
        conv_a = region_b[:, 2048:2048 + T]
        conv_b = region_b[:, 2560:2560 + T]
        soft = region_b[:, 0:KI * T].rearrange("p (m t) -> p m t", m=KI)
        attn_t = sb("attn_t", [P, KD, T])
        h1 = sb("h1", [S, 2, NB, D])
        h2 = sb("h2", [S, NB, D])
        u = sb("u", [P, KI, T])
        gate = sb("gate", [P, 2, KI, T])
        delta = sb("delta", [P, 2, KI, T])
        du = sb("du", [P, 2, KI, T])
        x_dbl = sb("x_dbl", [DT_RANK + 2 * NS, T])
        bc = sb("bc", [P, BC_SLOTS, 2, 2, T])
        decay = sb("decay", [P, DA_SLOTS, HT, T])
        work = sb("work", [P, W_SLOTS, HT, T])
        gelu = sb("gelu", [P, 2, T])
        square = sb("square", [P, T])
        sumsq = sb("sumsq", [P, T])
        row_max = sb("row_max", [S, 4])
        neg_max = sb("neg_max", [S, 2, 4])
        row_sum = sb("row_sum", [S, 2, 4])
        row_inv = sb("row_inv", [S, 4])
        stats = sb("stats", [S, NB, 6])
        mean_var = sb("mean_var", [S, NB, 2])
        var_in = sb("var_in", [S, 2, NB])
        root = sb("root", [S, 2, NB])
        denom = sb("denom", [S, NB])
        norm = sb("norm", [S, NB])
        mean_sq = sb("mean_sq", [S, NB])
        rms = sb("rms", [S, NB])
        rms_eps = sb("rms_eps", [S, NB])
        rms_inv = sb("rms_inv", [S, NB])

        y_acc = [ctx.enter_context(nc.psum_tensor(f"y_acc{m}", [P, 512], F32)) for m in range(KI)]
        ring = [ctx.enter_context(nc.psum_tensor(f"ring{m}", [P, 512], F32)) for m in range(SLOTS)]

        bc_dram = nc.dram_tensor("bc_scratch", [2, 2 * NS, T], F32, kind="Internal").ap()

        s_load = sem("s_load")
        s_pe = sem("s_pe")
        s_dve = sem("s_dve")
        s_pool = sem("s_pool")
        s_act = sem("s_act")
        s_tile = sem("s_tile")
        s_tile_act = sem("s_tile_act")
        s_tile_dve = sem("s_tile_dve")
        s_link = sem("s_link")
        s_plink = sem("s_plink")
        s_x = sem("s_x")
        s_bc = [sem(f"s_bc{i}") for i in range(BC_SLOTS)]
        s_bc_out = sem("s_bc_out")
        s_out = sem("s_out")
        s_z = sem("s_z")
        s_skip = sem("s_skip")
        s_decay = sem("s_decay")
        s_term = sem("s_term")
        s_state = sem("s_state")
        s_read = sem("s_read")
        s_pair = sem("s_pair")
        s_sum = sem("s_sum")
        s_var = sem("s_var")
        s_root = sem("s_root")
        s_xn = sem("s_xn")
        s_high = sem("s_high")
        s_gelu = sem("s_gelu")
        s_low = sem("s_low")
        s_sq = sem("s_sq")
        s_ms = sem("s_ms")
        s_nmax = sem("s_nmax")
        s_probs = sem("s_probs")
        s_conv = sem("s_conv")
        s_u = sem("s_u")
        s_abs = sem("s_abs")
        s_log = sem("s_log")
        clear = range(min(s.num for s in sems), max(s.num for s in sems) + 1)
        assert len(clear) == len(sems)

        tmp = [du, delta, gate]

        def scratch(i, lo, n, parts=P):
            return tmp[i][0:parts, :, :, :].rearrange("p a m t -> p (a m t)")[:, lo:lo + n]

        up_raw = work[:, :, :, :].rearrange("p a m t -> p (a m t)")[:, 0:KD * FF]
        down_raw = work[:, :, :, :].rearrange("p a m t -> p (a m t)")[:, 2048:2048 + KF * D]
        below = region_b[:, 0:2048]
        f2_nat = scratch(0, 0, KD * FF).rearrange("p (k f) -> p k f", k=KD)
        f2_t = scratch(1, 0, KF * D).rearrange("p (k f) -> p k f", k=KF)
        proj = scratch(2, 0, 1024).rearrange("p (k f) -> p k f", k=KD)
        proj_v = scratch(2, 1024, 512).rearrange("p (k f) -> p k f", k=KD)
        hw1 = scratch(2, 1536, 256).rearrange("p (k f) -> p k f", k=KD)
        fw1 = scratch(2, 1792, 256)
        hw2 = scratch(2, 2048, 256).rearrange("p (k f) -> p k f", k=KD)
        fw2 = scratch(2, 2304, 256)
        emb = scratch(2, 2560, KD * Z).rearrange("p (k z) -> p k z", k=KD)
        emb2 = scratch(2, 2900, KD * Z).rearrange("p (k z) -> p k z", k=KD)
        hid1 = scratch(2, 3240, Z)
        c1_rep = scratch(2, 3400, P)
        cols = scratch(2, 3540, 16)
        small = scratch(2, 3560, 16)
        rows = scratch(0, 3100, 768, 1)
        hid2 = region_a[:, 0:FF]

        loads = [
            (ident[:, :], "ident"), (emb[:, :, :], "emb"), (cols, "cols"), (hw1, "hw1"), (fw1, "fw1"),
            (proj, "proj"), (proj_v, "proj_v"), (rows, "rows"), (hw2, "hw2"), (fw2, "fw2"), (f2_nat, "f2_nat"),
            (f2_t, "f2_t"), (up_raw, "up"), (down_raw, "down"), (neg_a[:, :, :], "a_log"), (d_col[:, :], "d_col"),
            (w_f1[:, :, :], "f1"), (b_f1[:, :], "f1b"), (w_in[:, :, :], "w_in"), (w_conv[:, :, :], "w_conv"),
            (w_x[:, :, :], "w_x"), (w_dt[:, :], "w_dt"), (b_dt[:, :], "b_dt"), (w_out[:, :, :], "w_out"),
        ]
        with nc.Block() as block:
            @block.sync
            def _(sp):
                for dst, name in loads:
                    sp.dma_start(dst, ins[name]).then_inc(s_load, 16)
                sp.wait_ge(s_load, 16 * len(loads))

            @block.gpsimd
            def _(pool):
                nc.gpsimd.memset(decay[:, :, :, :], 0.0).then_inc(s_pool, 1)

            @block.scalar
            def _(act):
                act.wait_ge(s_load, 16 * len(loads))
                nc.scalar.activation(neg_a[:, :, :], neg_a[:, :, :], ACT.Exp).then_inc(s_act, 1)

            @block.tensor
            def _(pe):
                pe.wait_ge(s_load, 16 * len(loads))
                pe.wait_ge(s_dve, 2)
                for k in range(KD):
                    mm = nc.tensor.matmul(ring[0][:, 0:Z], hw1[:, k, :], emb[:, k, :], start=(k == 0),
                                          stop=(k == KD - 1))
                mm.then_inc(s_pe, 1)
                for k in range(KD):
                    for h in range(2):
                        mm = nc.tensor.matmul(ring[2 + h][:, :], hw2[:, k, :], f2_nat[:, k, h * 512:(h + 1) * 512],
                                              start=(k == 0), stop=(k == KD - 1))
                for k in range(KD):
                    mm = nc.tensor.matmul(y_acc[0][:, 0:1], hw2[:, k, :], cols[:, 10 + k:11 + k], start=(k == 0),
                                          stop=(k == KD - 1))
                mm.then_inc(s_pe, 1)
                for i in range(2):
                    pe.wait_ge(s_dve, 3 + i)
                    mm = nc.tensor.matmul(y_acc[1 + i][:, 0:1], ones[:, :], small[:, 1 + i:2 + i], start=True,
                                          stop=True)
                mm.then_inc(s_pe, 1)
                pe.wait_ge(s_dve, 5)
                for m in range(KD):
                    mm = nc.tensor.matmul(ring[m][:, 0:Z], fw1[:, m * P:(m + 1) * P], hid1, start=True, stop=True)
                mm.then_inc(s_pe, 1)
                pe.wait_ge(s_dve, 6)
                for m in range(4):
                    for k in range(KD):
                        mm = nc.tensor.matmul(ring[0][:, m * S:(m + 1) * S], proj[:, k, m * P:(m + 1) * P],
                                              emb2[:, k, PATCH:Z], start=(k == 0), stop=(k == KD - 1))
                for k in range(KD):
                    mm = nc.tensor.matmul(ring[1][0:PATCH, :], emb2[:, k, 0:PATCH], proj[:, k, :], start=(k == 0),
                                          stop=(k == KD - 1))
                mm.then_inc(s_pe, 1)
                pe.wait_ge(s_dve, 8)
                for k in range(KD):
                    mm = nc.tensor.matmul(y_acc[0][0:PATCH, 0:D], emb2[:, k, 0:PATCH], proj_v[:, k, :],
                                          start=(k == 0), stop=(k == KD - 1))
                for k in range(KD):
                    nc.tensor.matmul(y_acc[1][0:S, 0:D], emb2[:, k, PATCH:Z], proj_v[:, k, :], start=(k == 0),
                                     stop=False)
                nc.tensor.matmul(y_acc[1][0:S, 0:D], ones[0:1, 0:S], rows[0:1, 0:D], start=False, stop=True)
                nc.tensor.matmul(y_acc[2][0:S, 0:D], c1_rep[:, 0:S], fw2, start=True, stop=False)
                nc.tensor.matmul(y_acc[2][0:S, 0:D], ones[0:1, 0:S], rows[0:1, D:2 * D], start=False, stop=False)
                mm = nc.tensor.matmul(y_acc[2][0:S, 0:D], ones[0:1, 0:S], rows[0:1, 2 * D:3 * D], start=False,
                                      stop=True)
                mm.then_inc(s_pe, 1)
                for f in range(KF):
                    if f >= 2:
                        pe.wait_ge(s_dve, 8 + f - 1)
                    nc.tensor.matmul(ring[2 + f % 2][:, 0:D], hid2[:, f * P:(f + 1) * P], fw2, start=True,
                                     stop=True).then_inc(s_pe, 1)

            @block.vector
            def _(dve):
                linked = [0]

                def link(ins_):
                    linked[0] += 1
                    ins_.then_inc(s_link, 1)
                    dve.wait_ge(s_link, linked[0])

                nc.vector.memset(ones[:, :], 1.0)
                nc.vector.memset(half[:, :], 0.5)
                nc.vector.memset(minus_half[:, :], -0.5).then_inc(s_dve, 1)
                dve.wait_ge(s_load, 16 * len(loads))
                for k in range(KD):
                    ins_ = nc.vector.tensor_scalar(emb[:, k, PATCH:Z], emb[:, k, PATCH:Z], cols[:, k:k + 1], None,
                                                   ALU.add)
                ins_.then_inc(s_dve, 1)
                for i, w in enumerate((up_raw, down_raw)):
                    nc.vector.tensor_reduce(small[:, 1 + i:2 + i], w, AX.X, ALU.add,
                                            apply_absolute_value=True).then_inc(s_dve, 1)
                dve.wait_ge(s_pe, 1)
                nc.vector.tensor_copy(hid1[:, 0:PATCH], ring[0][:, 0:PATCH])
                nc.vector.tensor_scalar(hid1[:, PATCH:Z], ring[0][:, PATCH:Z], cols[:, 2:3], None,
                                        ALU.add).then_inc(s_dve, 1)
                dve.wait_ge(s_pe, 4)
                for m in range(KD):
                    link(nc.vector.tensor_tensor(emb2[:, m, :], ring[m][:, 0:Z], emb[:, m, :], ALU.add))
                    ins_ = nc.vector.tensor_scalar(emb2[:, m, PATCH:Z], emb2[:, m, PATCH:Z], cols[:, 3 + m:4 + m],
                                                   None, ALU.add)
                ins_.then_inc(s_dve, 1)
                nc.vector.tensor_copy(hid2[:, 0:512], ring[2][:, :])
                nc.vector.tensor_copy(hid2[:, 512:1024], ring[3][:, :]).then_inc(s_dve, 1)
                link(nc.vector.tensor_scalar(small[:, 0:1], y_acc[0][:, 0:1], cols[:, 9:10], None, ALU.add))
                nc.vector.tensor_scalar(c1_rep, ones[:, :], small[:, 0:1], None, ALU.mult)
                for i in range(2):
                    nc.vector.tensor_scalar(small[:, 3 + i:4 + i], y_acc[1 + i][:, 0:1], 0.5 / (D * FF), None, ALU.mult)
                    ins_ = nc.vector.tensor_scalar(small[:, 5 + i:6 + i], y_acc[1 + i][:, 0:1], -0.5 / (D * FF), None,
                                                   ALU.mult)
                ins_.then_inc(s_dve, 1)
                dve.wait_ge(s_dve, 8)
                for f in range(KF):
                    dve.wait_ge(s_pe, 7 + f)
                    nc.vector.tensor_tensor(w_f2[:, f, :], ring[2 + f % 2][:, 0:D], f2_t[:, f, :],
                                            ALU.add).then_inc(s_dve, 1)
                for i, (w, dst) in enumerate(((up_raw, w_up), (down_raw, w_down))):
                    flat = dst[:, :, :].rearrange("p a b -> p (a b)")
                    link(nc.vector.tensor_scalar(below, w, small[:, 5 + i:6 + i], None, ALU.is_lt))
                    link(nc.vector.scalar_tensor_tensor(out=flat, in0=w, scalar=small[:, 3 + i:4 + i], in1=below,
                                                        op0=ALU.is_gt, op1=ALU.subtract))
                for m in range(4):
                    nc.vector.tensor_scalar(pos_qk[:, m, :], ring[0][:, m * S:(m + 1) * S], cols[:, 5 + m:6 + m], None,
                                            ALU.add)
                nc.vector.tensor_copy(w_qk[:, :], ring[1][0:PATCH, :])
                nc.vector.tensor_copy(w_v[:, :], y_acc[0][0:PATCH, 0:D])
                nc.vector.tensor_copy(pos_v[:, :], y_acc[1][0:S, 0:D])
                nc.vector.tensor_copy(b_f2[:, :], y_acc[2][0:S, 0:D])
                for m in range(KI):
                    nc.vector.tensor_scalar(d_diag[:, m, :], ident[:, :], d_col[:, m:m + 1], None, ALU.mult)
                dve.wait_ge(s_act, 1)
                link(nc.vector.tensor_scalar(neg_a[:, :, :], neg_a[:, :, :], -1.0, None, ALU.mult))
        nc.all_engine_barrier(sems_to_clear=clear)

        def step(c, scan, post, pre, x_cols=None, out_rows=None):
            o = 1 - c
            at, tile, freed, frees = schedule(post, pre)
            pair_of = [(j // 4, (j // 2) % 2, 2 * (j // 4) + j % 2) for j in range(UNITS)]

            def wait_freed(eng, name, i):
                who, n = freed[name, i]
                eng.wait_ge(s_tile_act if who == "act" else s_tile_dve, n)

            def wait_tile(eng, name, i):
                eng.wait_ge(s_tile, tile[name, i] + 1)

            def bank(name, i):
                return ring[tile[name, i] % SLOTS]

            def wait_bank(eng, name, i):
                t = tile[name, i]
                if t >= SLOTS:
                    who, n = frees[t - SLOTS]
                    eng.wait_ge(s_tile_act if who == "act" else s_tile_dve, n)

            with nc.Block() as block:
                @block.sync
                def _(sp):
                    if pre:
                        sp.dma_start(patches[:, :], x_cols).then_inc(s_x, 16)
                    if scan:
                        for p in range(PAIRS):
                            if p >= BC_SLOTS:
                                sp.wait_ge(s_read, 4 * (p - BC_SLOTS + 1))
                                sp.wait_ge(s_term, 4 * (p - BC_SLOTS + 1))
                            for i in range(2):
                                src = bc_dram[c, NS * i + 2 * p:NS * i + 2 * p + 2, :]
                                src = src.rearrange("n t -> (n t)").unsqueeze(0).to_broadcast([P, 2 * T])
                                sp.dma_start(bc[:, p % BC_SLOTS, i].rearrange("p n t -> p (n t)"),
                                             src).then_inc(s_bc[p % BC_SLOTS], 16)
                    if pre:
                        wait_freed(sp, "w_x", 0)
                        sp.dma_start(bc_dram[o], x_dbl[DT_RANK:DT_RANK + 2 * NS, :]).then_inc(s_bc_out, 16)
                        sp.wait_ge(s_bc_out, 16)
                        sp.wait_ge(s_x, 16)

                @block.gpsimd
                def _(pool):
                    linked = [0]

                    def link(ins_):
                        linked[0] += 1
                        ins_.then_inc(s_plink, 1)
                        pool.wait_ge(s_plink, linked[0])

                    def term(j):
                        p, h, n = pair_of[j]
                        pool.wait_ge(s_bc[p % BC_SLOTS], 32 * (p // BC_SLOTS + 1))
                        if j >= W_SLOTS:
                            pool.wait_ge(s_sum, (j - W_SLOTS) // 2 + 1)
                        nc.gpsimd.tensor_tensor(
                            work[:, j % W_SLOTS], du[:, c, HT * h:HT * h + HT, :],
                            bc[:, p % BC_SLOTS, 0, n % 2].unsqueeze(1).to_broadcast([P, HT, T]),
                            ALU.mult).then_inc(s_term, 1)

                    def norm2(i):
                        pool.wait_ge(s_var, 1)
                        nc.gpsimd.tensor_tensor(root[:, :, :], var_in[:, :, :],
                                                half[:, :].rearrange("p (a b) -> p a b", a=2),
                                                ALU.pow).then_inc(s_root, 1)

                    def norm1(i):
                        pool.wait_ge(s_var, 1 + post)
                        nc.gpsimd.tensor_tensor(norm[:, :], var_in[:, 1, :], minus_half[:, :],
                                                ALU.pow).then_inc(s_root, 1)

                    def up(m):
                        wait_freed(pool, "up", m)
                        if m == 0:
                            nc.gpsimd.tensor_tensor(sumsq[:, :], gelu[:, 0], gelu[:, 0], ALU.mult).then_inc(s_sq, 1)
                            return
                        pool.wait_ge(s_sq, m)
                        link(nc.gpsimd.tensor_tensor(square[:, :], gelu[:, m % 2], gelu[:, m % 2], ALU.mult))
                        nc.gpsimd.tensor_tensor(sumsq[:, :], sumsq[:, :], square[:, :], ALU.add).then_inc(s_sq, 1)

                    def sumsq_(i):
                        wait_freed(pool, "sumsq", 0)
                        nc.gpsimd.tensor_tensor(rms[:, :], mean_sq[:, :], half[:, 0:NB], ALU.pow).then_inc(s_ms, 1)

                    stages = dict(norm2=norm2, norm1=norm1, up=up, sumsq=sumsq_)
                    for j in range(UNITS):
                        if scan:
                            term(j)
                        for name, i in at[j]:
                            if name in stages:
                                stages[name](i)

                @block.scalar
                def _(act):
                    def decays(j):
                        p, h, n = pair_of[j]
                        if j >= DA_SLOTS:
                            act.wait_ge(s_state, j - DA_SLOTS + 1)
                        for m in range(HT):
                            dst = decay[:, j % DA_SLOTS, m].rearrange("p (b t) -> p b t", b=NB)[:, :, 1:S]
                            src = delta[:, c, HT * h + m].rearrange("p (b t) -> p b t", b=NB)[:, :, 1:S]
                            ins_ = nc.scalar.activation(dst, src, ACT.Exp, scale=neg_a[:, HT * h + m, n:n + 1])
                        ins_.then_inc(s_decay, 1)

                    def turn2(k):
                        wait_tile(act, "turn2", k)
                        nc.scalar.activation(xn_parts[:, 0, k], bank("turn2", k)[:, 0:T], ACT.Copy).then_inc(s_high, 1)

                    def up(m):
                        wait_tile(act, "up", m)
                        if m >= 2:
                            act.wait_ge(s_low, m - 1)
                            act.wait_ge(s_sq, m - 1)
                        nc.scalar.activation(g_parts[:, 0, m], bank("up", m)[:, 0:T], ACT.Gelu).then_inc(s_gelu, 1)
                        nc.scalar.activation(gelu[:, m % 2], bank("up", m)[:, 0:T], ACT.Gelu).then_inc(s_tile_act, 1)

                    def score(i):
                        wait_tile(act, "score", i)
                        act.wait_ge(s_nmax, i + 1)
                        if i >= 2:
                            wait_tile(act, "turn_p", i - 2)
                            act.wait_ge(s_probs, i - 1)
                        for q in range(4):
                            ins_ = nc.scalar.activation(probs[:, i % 2, q], bank("score", i)[0:S, q * S:(q + 1) * S],
                                                        ACT.Exp, bias=neg_max[:, i % 2, q:q + 1], scale=DK ** -0.5,
                                                        accum_out=row_sum[:, i % 2, q:q + 1])
                        ins_.then_inc(s_tile_act, 1)

                    def turn_p(i):
                        wait_tile(act, "turn_p", i)
                        if i >= 2:
                            wait_tile(act, "pv", i // 2 - 1)
                        nc.scalar.activation(probs_t[:, i % 2].rearrange("p c t -> p (c t)"),
                                             bank("turn_p", i)[0:S, 0:T], ACT.Copy).then_inc(s_tile_act, 1)

                    def pv(i):
                        wait_tile(act, "pv", i)
                        nc.scalar.activation(attn_t[:, :, 2 * S * i:2 * S * (i + 1)],
                                             bank("pv", i)[:, 0:T].rearrange("p (k t) -> p k t", k=KD),
                                             ACT.Copy).then_inc(s_tile_act, 1)

                    def f1(m):
                        wait_tile(act, "f1", m)
                        nc.scalar.activation(relu[:, m], bank("f1", m)[:, 0:T], ACT.Relu,
                                             bias=b_f1[:, m:m + 1]).then_inc(s_tile_act, 1)

                    def turn1(k):
                        wait_tile(act, "turn1", k)
                        nc.scalar.activation(xn_t[:, k], bank("turn1", k)[:, 0:T], ACT.Copy).then_inc(s_tile_act, 1)

                    def w_in_(m):
                        wait_tile(act, "w_in", m)
                        src = bank("w_in", m)[:, 0:T]
                        if m < KI:
                            nc.scalar.activation(padded[:, m, :, 2:S + 2], src.rearrange("p (b t) -> p b t", b=NB),
                                                 ACT.Copy).then_inc(s_tile_act, 1)
                        else:
                            if post:
                                act.wait_ge(s_z, 4)
                            nc.scalar.activation(gate[:, o, m - KI], src, ACT.Silu).then_inc(s_tile_act, 1)

                    def silu(m):
                        act.wait_ge(s_conv, m + 1)
                        nc.scalar.activation(u[:, m], u[:, m], ACT.Silu).then_inc(s_u, 1)

                    def w_x_(i):
                        wait_tile(act, "w_x", 0)
                        nc.scalar.activation(x_dbl[:, :], bank("w_x", 0)[0:DT_RANK + 2 * NS, 0:T],
                                             ACT.Copy).then_inc(s_tile_act, 1)

                    def w_dt_(m):
                        wait_tile(act, "w_dt", m)
                        act.wait_ge(s_conv, KI)
                        nc.scalar.activation(soft[:, m], bank("w_dt", m)[:, 0:T], ACT.Abs,
                                             bias=b_dt[:, m:m + 1]).then_inc(s_abs, 1)

                    def delta_(i):
                        act.wait_ge(s_abs, KI)
                        nc.scalar.activation(soft, soft, ACT.Exp, scale=-1.0).then_inc(s_abs, 1)
                        act.wait_ge(s_abs, KI + 1)
                        nc.scalar.activation(soft, soft, ACT.Ln, bias=1.0).then_inc(s_log, 1)

                    stages = dict(turn2=turn2, up=up, score=score, turn_p=turn_p, pv=pv, f1=f1, turn1=turn1,
                                  w_in=w_in_, silu=silu, w_x=w_x_, w_dt=w_dt_, delta=delta_)
                    for j in range(UNITS):
                        if scan:
                            decays(j)
                        for name, i in at[j]:
                            if name in stages:
                                stages[name](i)
                    if post:
                        wait_freed(act, "down", 1)
                        act.dma_start(out_rows, h2[:, :, :]).then_inc(s_out, 16)
                        act.wait_ge(s_out, 16)

                @block.tensor
                def _(pe):
                    def skip():
                        for m in range(KI):
                            if post:
                                pe.wait_ge(s_z, m + 1)
                            ins_ = nc.tensor.matmul(y_acc[m][:, 0:T], d_diag[:, m, :], u[:, m], start=True,
                                                    stop=False, skip_group_check=True)
                        ins_.then_inc(s_skip, 1)

                    def add_pair(q):
                        pe.wait_ge(s_pair, q + 1)
                        for m in range(HT):
                            ins_ = nc.tensor.matmul(y_acc[HT * (q % 2) + m][:, 0:T], ident[:, :],
                                                    work[:, (2 * q) % W_SLOTS, m], start=False, stop=(q >= NS - 2),
                                                    skip_group_check=True)
                        ins_.then_inc(s_sum, 1)

                    def w_out_(i):
                        pe.wait_ge(s_z, 4)
                        wait_bank(pe, "w_out", i)
                        for b in range(2):
                            t0 = (2 * i + b) * S
                            for k in range(KI):
                                mm = nc.tensor.matmul(bank("w_out", i)[0:S, b * D:(b + 1) * D],
                                                      gated[:, k, t0:t0 + S], w_out[:, k, :], start=(k == 0),
                                                      stop=(k == KI - 1))
                        mm.then_inc(s_tile, 1)

                    def turn(name, k):
                        wait_bank(pe, name, k)
                        for b in range(NB):
                            mm = nc.tensor.transpose(bank(name, k)[:, b * S:(b + 1) * S],
                                                     xn[:, b, k * P:(k + 1) * P], ident[0:S, 0:S])
                        mm.then_inc(s_tile, 1)

                    def turn2(k):
                        pe.wait_ge(s_xn, NB)
                        turn("turn2", k)

                    def turn1(k):
                        pe.wait_ge(s_xn, NB * (1 + post))
                        turn("turn1", k)

                    def up(m):
                        wait_freed(pe, "turn2", 1)
                        wait_bank(pe, "up", m)
                        for k in range(KD):
                            for part in range(2):
                                mm = nc.tensor.matmul(bank("up", m)[:, 0:T], w_up[:, k, m * P:(m + 1) * P],
                                                      xn_parts[:, part, k], start=(k == 0 and part == 0),
                                                      stop=(k == KD - 1 and part == 1))
                        mm.then_inc(s_tile, 1)

                    def sumsq_(i):
                        pe.wait_ge(s_sq, KF)
                        wait_bank(pe, "sumsq", 0)
                        for b in range(NB):
                            mm = nc.tensor.matmul(bank("sumsq", 0)[0:S, b:b + 1], sumsq[:, b * S:(b + 1) * S],
                                                  ones[:, 0:1], start=True, stop=True)
                        mm.then_inc(s_tile, 1)

                    def down(i):
                        pe.wait_ge(s_low, KF)
                        wait_bank(pe, "down", i)
                        for b in range(2):
                            t0 = (2 * i + b) * S
                            for m in range(KF):
                                for part in range(2):
                                    mm = nc.tensor.matmul(bank("down", i)[0:S, b * D:(b + 1) * D],
                                                          g_parts[:, part, m, t0:t0 + S], w_down[:, m, :],
                                                          start=(m == 0 and part == 0),
                                                          stop=(m == KF - 1 and part == 1))
                        mm.then_inc(s_tile, 1)

                    def qk_(m):
                        pe.wait_ge(s_x, 16)
                        wait_bank(pe, "qk", m)
                        nc.tensor.matmul(bank("qk", m)[:, 0:T], w_qk[:, m * P:(m + 1) * P], patches[:, :], start=True,
                                         stop=True).then_inc(s_tile, 1)

                    def v_(i):
                        wait_bank(pe, "v", i)
                        for b in range(2):
                            t0 = (2 * i + b) * S
                            mm = nc.tensor.matmul(bank("v", i)[0:S, b * D:(b + 1) * D], patches[:, t0:t0 + S],
                                                  w_v[:, :], start=True, stop=True)
                        mm.then_inc(s_tile, 1)

                    def score(i):
                        wait_freed(pe, "qk", 3)
                        wait_bank(pe, "score", i)
                        r = DK * (i % 2)
                        for hh in range(2):
                            for b in range(2):
                                t0 = (2 * (i // 2) + b) * S
                                q = 2 * hh + b
                                mm = nc.tensor.matmul(bank("score", i)[0:S, q * S:(q + 1) * S],
                                                      qk[r:r + DK, hh, t0:t0 + S], qk[r:r + DK, 2 + hh, t0:t0 + S],
                                                      start=True, stop=True)
                        mm.then_inc(s_tile, 1)

                    def turn_p(i):
                        pe.wait_ge(s_probs, i + 1)
                        wait_bank(pe, "turn_p", i)
                        for q in range(4):
                            mm = nc.tensor.transpose(bank("turn_p", i)[0:S, q * S:(q + 1) * S], probs[:, i % 2, q],
                                                     ident[0:S, 0:S])
                        mm.then_inc(s_tile, 1)

                    def pv(i):
                        wait_freed(pe, "turn_p", 2 * i + 1)
                        wait_freed(pe, "v", 1)
                        wait_bank(pe, "pv", i)
                        for odd in range(2):
                            for hh in range(2):
                                for b in range(2):
                                    q = 2 * hh + b
                                    h0 = (2 * hh + odd) * DK
                                    mm = nc.tensor.matmul(bank("pv", i)[DK * odd:DK * (odd + 1), q * S:(q + 1) * S],
                                                          v_tok[:, 2 * i + b, h0:h0 + DK], probs_t[:, odd, q],
                                                          start=True, stop=True)
                        mm.then_inc(s_tile, 1)

                    def f1(m):
                        wait_freed(pe, "pv", 1)
                        wait_bank(pe, "f1", m)
                        for k in range(KD):
                            mm = nc.tensor.matmul(bank("f1", m)[:, 0:T], w_f1[:, k, m * P:(m + 1) * P], attn_t[:, k],
                                                  start=(k == 0), stop=(k == KD - 1))
                        mm.then_inc(s_tile, 1)

                    def f2(i):
                        wait_freed(pe, "f1", KF - 1)
                        wait_bank(pe, "f2", i)
                        for b in range(2):
                            t0 = (2 * i + b) * S
                            for m in range(KF):
                                mm = nc.tensor.matmul(bank("f2", i)[0:S, b * D:(b + 1) * D], relu[:, m, t0:t0 + S],
                                                      w_f2[:, m, :], start=(m == 0), stop=(m == KF - 1))
                        mm.then_inc(s_tile, 1)

                    def w_in_(m):
                        wait_freed(pe, "turn1", 1)
                        wait_bank(pe, "w_in", m)
                        for k in range(KD):
                            mm = nc.tensor.matmul(bank("w_in", m)[:, 0:T], w_in[:, k, m * P:(m + 1) * P], xn_t[:, k],
                                                  start=(k == 0), stop=(k == KD - 1))
                        mm.then_inc(s_tile, 1)

                    def w_x_(i):
                        pe.wait_ge(s_u, KI)
                        wait_bank(pe, "w_x", 0)
                        for k in range(KI):
                            mm = nc.tensor.matmul(bank("w_x", 0)[0:DT_RANK + 2 * NS, 0:T], w_x[:, k, :], u[:, k],
                                                  start=(k == 0), stop=(k == KI - 1))
                        mm.then_inc(s_tile, 1)

                    def w_dt_(m):
                        wait_freed(pe, "w_x", 0)
                        wait_bank(pe, "w_dt", m)
                        nc.tensor.matmul(bank("w_dt", m)[:, 0:T], w_dt[:, m * P:(m + 1) * P], x_dbl[0:DT_RANK, :],
                                         start=True, stop=True).then_inc(s_tile, 1)

                    stages = dict(w_out=w_out_, turn2=turn2, up=up, sumsq=sumsq_, down=down, qk=qk_, v=v_, score=score,
                                  turn_p=turn_p, pv=pv, f1=f1, f2=f2, turn1=turn1, w_in=w_in_, w_x=w_x_, w_dt=w_dt_)
                    for j in range(UNITS):
                        if scan and j == 0:
                            skip()
                        if scan and j >= 3 and j % 2 == 1:
                            add_pair((j - 3) // 2)
                        for name, i in at[j]:
                            if name in stages:
                                stages[name](i)
                    if scan:
                        add_pair(NS - 1)

                @block.vector
                def _(dve):
                    linked = [0]

                    def link(ins_):
                        linked[0] += 1
                        ins_.then_inc(s_link, 1)
                        dve.wait_ge(s_link, linked[0])

                    def state(j):
                        dve.wait_ge(s_decay, j + 1)
                        dve.wait_ge(s_term, j + 1)
                        w = work[:, j % W_SLOTS].rearrange("p m t -> p (m t)")
                        nc.vector.tensor_tensor_scan(w, decay[:, j % DA_SLOTS].rearrange("p m t -> p (m t)"), w, 0.0,
                                                     ALU.mult, ALU.add).then_inc(s_state, 1)

                    def read(j):
                        p, h, n = pair_of[j]
                        dve.wait_ge(s_state, j + 1)
                        w = work[:, j % W_SLOTS]
                        nc.vector.tensor_tensor(w, w, bc[:, p % BC_SLOTS, 1, n % 2].unsqueeze(1).to_broadcast(
                            [P, HT, T]), ALU.mult).then_inc(s_read, 1)

                    def add(j):
                        dve.wait_ge(s_read, j + 1)
                        first = work[:, (j - 1) % W_SLOTS]
                        nc.vector.tensor_tensor(first, first, work[:, j % W_SLOTS], ALU.add).then_inc(s_pair, 1)

                    def z(m):
                        nc.vector.tensor_tensor(gated[:, m], y_acc[m][:, 0:T], gate[:, o, m],
                                                ALU.mult).then_inc(s_z, 1)

                    def w_out_(i):
                        wait_tile(dve, "w_out", i)
                        nc.vector.tensor_tensor(h2[:, 2 * i:2 * i + 2, :],
                                                bank("w_out", i)[0:S, :].rearrange("p (b d) -> p b d", b=2),
                                                h1[:, o, 2 * i:2 * i + 2, :], ALU.add).then_inc(s_tile_dve, 1)

                    def moments(h):
                        for b in range(NB):
                            ins_ = nc.vector.bn_stats(stats[:, b, :], h[:, b, :])
                        link(ins_)
                        for b in range(NB):
                            ins_ = nc.vector.bn_aggr(mean_var[:, b, :], stats[:, b, :])
                        link(ins_)

                    def normed(h, scale):
                        for b in range(NB):
                            nc.vector.tensor_scalar(xn[:, b, :], h[:, b, :], mean_var[:, b, 0:1], scale[:, b:b + 1],
                                                    ALU.subtract, ALU.mult).then_inc(s_xn, 1)

                    def norm2(i):
                        wait_freed(dve, "w_out", 1)
                        moments(h2)
                        nc.vector.tensor_copy(var_in[:, 0, :], mean_var[:, :, 1])
                        nc.vector.tensor_scalar(var_in[:, 1, :], mean_var[:, :, 1], LN_EPS, None,
                                                ALU.add).then_inc(s_var, 1)
                        dve.wait_ge(s_root, 1)
                        link(nc.vector.scalar_tensor_tensor(out=denom[:, :], in0=root[:, 1, :], scalar=RMS_EPS,
                                                            in1=root[:, 0, :], op0=ALU.mult, op1=ALU.add))
                        link(nc.vector.reciprocal(denom[:, :], denom[:, :]))
                        normed(h2, denom)

                    def norm1(i):
                        wait_freed(dve, "f2", 1)
                        moments(h1[:, o])
                        nc.vector.tensor_scalar(var_in[:, 1, :], mean_var[:, :, 1], LN_EPS, None,
                                                ALU.add).then_inc(s_var, 1)
                        nc.vector.memset(padded[:, :, :, 0:2], 0.0)
                        dve.wait_ge(s_root, 1 + post)
                        normed(h1[:, o], norm)

                    def turn2(k):
                        dve.wait_ge(s_high, k + 1)
                        nc.vector.tensor_tensor(xn_parts[:, 1, k], bank("turn2", k)[:, 0:T], xn_parts[:, 0, k],
                                                ALU.subtract).then_inc(s_tile_dve, 1)

                    def up(m):
                        wait_freed(dve, "up", m)
                        nc.vector.tensor_tensor(g_parts[:, 1, m], gelu[:, m % 2], g_parts[:, 0, m],
                                                ALU.subtract).then_inc(s_low, 1)

                    def sumsq_(i):
                        wait_tile(dve, "sumsq", 0)
                        nc.vector.tensor_scalar(mean_sq[:, :], bank("sumsq", 0)[0:S, 0:NB], 1.0 / FF, None,
                                                ALU.mult).then_inc(s_tile_dve, 1)

                    def down(i):
                        if i == 0:
                            dve.wait_ge(s_ms, 1)
                            link(nc.vector.tensor_scalar(rms_eps[:, :], rms[:, :], RMS_EPS, None, ALU.add))
                            link(nc.vector.reciprocal(rms_inv[:, :], rms_eps[:, :]))
                        wait_tile(dve, "down", i)
                        for b in range(2):
                            s = 2 * i + b
                            ins_ = nc.vector.scalar_tensor_tensor(
                                out=h2[:, s, :], in0=bank("down", i)[0:S, b * D:(b + 1) * D],
                                scalar=rms_inv[:, s:s + 1], in1=h2[:, s, :], op0=ALU.mult, op1=ALU.add)
                        ins_.then_inc(s_tile_dve, 1)

                    def qk_(m):
                        if post:
                            wait_tile(dve, "up", KF - 1)
                        wait_tile(dve, "qk", m)
                        nc.vector.tensor_tensor(
                            qk[:, m].rearrange("p (b t) -> p b t", b=NB),
                            bank("qk", m)[:, 0:T].rearrange("p (b t) -> p b t", b=NB),
                            pos_qk[:, m].unsqueeze(1).to_broadcast([P, NB, S]), ALU.add).then_inc(s_tile_dve, 1)

                    def v_(i):
                        wait_tile(dve, "v", i)
                        nc.vector.tensor_tensor(
                            v_tok[:, 2 * i:2 * i + 2, :], bank("v", i)[0:S, :].rearrange("p (b d) -> p b d", b=2),
                            pos_v[:, :].unsqueeze(1).to_broadcast([S, 2, D]), ALU.add).then_inc(s_tile_dve, 1)

                    def score(i):
                        wait_tile(dve, "score", i)
                        if i >= 2:
                            wait_freed(dve, "score", i - 2)
                        if i >= 1:
                            dve.wait_ge(s_nmax, i)
                        link(nc.vector.tensor_reduce(row_max[:, :],
                                                     bank("score", i)[0:S, 0:T].rearrange("p (q t) -> p q t", q=4),
                                                     AX.X, ALU.max))
                        nc.vector.tensor_scalar(neg_max[:, i % 2, :], row_max[:, :], -DK ** -0.5, None,
                                                ALU.mult).then_inc(s_nmax, 1)

                    def turn_p(i):
                        wait_freed(dve, "score", i)
                        if i >= 1:
                            dve.wait_ge(s_probs, i)
                        link(nc.vector.reciprocal(row_inv[:, :], row_sum[:, i % 2, :]))
                        nc.vector.tensor_tensor(probs[:, i % 2], probs[:, i % 2],
                                                row_inv[:, :].unsqueeze(2).to_broadcast([S, 4, S]),
                                                ALU.mult).then_inc(s_probs, 1)

                    def f2(i):
                        wait_tile(dve, "f2", i)
                        nc.vector.tensor_tensor(h1[:, o, 2 * i:2 * i + 2, :],
                                                bank("f2", i)[0:S, :].rearrange("p (b d) -> p b d", b=2),
                                                b_f2[:, :].unsqueeze(1).to_broadcast([S, 2, D]),
                                                ALU.add).then_inc(s_tile_dve, 1)

                    def w_in_(m):
                        if m >= KI:
                            return
                        wait_freed(dve, "w_in", m)
                        if m >= 1:
                            dve.wait_ge(s_conv, m)
                        if scan and m == 0:
                            dve.wait_ge(s_skip, 1)

                        def seqs(a):
                            return a.rearrange("p (b t) -> p b t", b=NB)

                        link(nc.vector.tensor_scalar(seqs(conv_a), padded[:, m, :, 0:S], w_conv[:, m, 0:1], None,
                                                     ALU.mult))
                        link(nc.vector.scalar_tensor_tensor(out=seqs(conv_b), in0=padded[:, m, :, 1:S + 1],
                                                            scalar=w_conv[:, m, 1:2], in1=seqs(conv_a), op0=ALU.mult,
                                                            op1=ALU.add))
                        nc.vector.scalar_tensor_tensor(out=seqs(u[:, m]), in0=padded[:, m, :, 2:S + 2],
                                                       scalar=w_conv[:, m, 2:3], in1=seqs(conv_b), op0=ALU.mult,
                                                       op1=ALU.add).then_inc(s_conv, 1)

                    def w_dt_(m):
                        dve.wait_ge(s_abs, m + 1)
                        nc.vector.tensor_scalar(delta[:, o, m], bank("w_dt", m)[:, 0:T], b_dt[:, m:m + 1], 0.0,
                                                ALU.add, ALU.max).then_inc(s_tile_dve, 1)

                    def delta_(i):
                        dve.wait_ge(s_log, 1)
                        wait_freed(dve, "w_dt", KI - 1)
                        link(nc.vector.tensor_tensor(delta[:, o], delta[:, o], soft, ALU.add))
                        link(nc.vector.tensor_tensor(du[:, o], delta[:, o], u[:, :, :], ALU.mult))

                    stages = dict(z=z, w_out=w_out_, norm2=norm2, turn2=turn2, up=up, sumsq=sumsq_, down=down, qk=qk_,
                                  v=v_, score=score, turn_p=turn_p, f2=f2, norm1=norm1, w_in=w_in_, w_dt=w_dt_,
                                  delta=delta_)
                    for j in range(UNITS):
                        if scan:
                            if j == 0:
                                for name, i in at[j]:
                                    if name == "z":
                                        z(i)
                            state(j)
                            if j >= 1:
                                read(j - 1)
                            if j >= 2 and j % 2 == 0:
                                add(j - 1)
                        for name, i in at[j]:
                            if name in stages and not (scan and j == 0 and name == "z"):
                                stages[name](i)
                    if scan:
                        read(UNITS - 1)
                        add(UNITS - 1)

            nc.all_engine_barrier(sems_to_clear=clear)

        x_t = ins["x_t"]
        out_g = out.rearrange("(g b) s d -> g s b d", b=NB)
        x_g = x_t.rearrange("c (g t) -> g c t", g=GROUPS)
        step(1, False, False, True, x_g[0])
        step(0, True, False, True, x_g[1])
        with nc.Fori(0, (GROUPS - 2) // 2) as i:
            step(1, True, True, True, x_g[bass.ds(2 * i + 2, 1)], out_g[bass.ds(2 * i, 1)])
            step(0, True, True, True, x_g[bass.ds(2 * i + 3, 1)], out_g[bass.ds(2 * i + 1, 1)])
        step(1, True, True, False, None, out_g[GROUPS - 2])
        step(0, False, True, False, None, out_g[GROUPS - 1])


def positions():
    pos = np.arange(S, dtype=np.float32)[:, None]
    div = np.exp(np.arange(0, D, 2, dtype=np.float32) * np.float32(-np.log(10000.0) / D))
    ang = pos * div
    return np.stack([np.sin(ang), np.cos(ang)], axis=-1).reshape(S, D).astype(np.float32)


def tiles(a):
    return np.ascontiguousarray(a.reshape(-1, P, a.shape[-1]).transpose(1, 0, 2))


def column(a):
    return np.ascontiguousarray(a.reshape(-1, P).T)


def kernel(**inputs):
    import concourse.bacc as bacc
    from concourse.bass_utils import run_bass_kernel_spmd

    v = {k: np.asarray(a) for k, a in inputs.items()}
    tok = {k[7:]: a for k, a in v.items() if k.startswith("L0_tok_")}
    ssm = {k[8:]: a for k, a in v.items() if k.startswith("L0_attn_")}
    flat = {k: tok[k].reshape(D, D) for k in ("Wq", "Wk", "Wv")}
    cols = np.concatenate([column(tok["bp"]), column(tok["rb1_hb"]), column(tok["rb1_fb"]),
                           column(tok["bq"].reshape(-1)), column(tok["bk"].reshape(-1)), column(tok["rb2_hb"]),
                           column(tok["f2b"]), np.zeros((P, 4), np.float32)], axis=1)
    arrays = {
        "x_t": v["x"].reshape(B * S, PATCH).T,
        "ident": np.eye(P, dtype=np.float32),
        "emb": tiles(np.concatenate([tok["Wp"], positions().T], axis=1)),
        "cols": cols,
        "hw1": tiles(tok["rb1_hw"].T), "fw1": tok["rb1_fw"].T,
        "proj": tiles(np.concatenate([flat["Wq"].T, flat["Wk"].T], axis=1)), "proj_v": tiles(flat["Wv"].T),
        "rows": np.concatenate([tok["bv"].reshape(-1), tok["f2b"], tok["rb2_fb"]])[None, :],
        "hw2": tiles(tok["rb2_hw"].T), "fw2": tok["rb2_fw"].T,
        "f2_nat": tiles(tok["f2w"]), "f2_t": tiles(tok["f2w"].T),
        "up": tiles(v["L0_ffn_w_up"].T).reshape(P, -1), "down": tiles(v["L0_ffn_w_down"].T).reshape(P, -1),
        "a_log": tiles(ssm["A_log"]), "d_col": column(ssm["D_param"]),
        "f1": tiles(tok["f1w"].T), "f1b": column(tok["f1b"]),
        "w_in": tiles(ssm["W_in"]), "w_conv": tiles(ssm["W_conv"]), "w_x": tiles(ssm["W_x"]), "w_dt": ssm["W_dt"],
        "b_dt": column(ssm["b_dt"]), "w_out": tiles(ssm["W_out"]),
    }
    nc = bacc.Bacc("TRN2", target_bir_lowering=False, num_devices=1)
    feeds, aps = {}, {}
    for name, a in arrays.items():
        a = np.ascontiguousarray(a)
        feeds[f"in_{name}"] = a
        aps[name] = nc.dram_tensor(f"in_{name}", a.shape, mybir.dt.from_np(a.dtype), kind="ExternalInput").ap()
    out = nc.dram_tensor("out_0", (B, S, D), F32, kind="ExternalOutput").ap()
    build(nc, aps, out)
    r = run_bass_kernel_spmd(nc, [feeds], core_ids=[0])
    return r.results[0]["out_0"]
```

```python
from contextlib import ExitStack

import numpy as np

import concourse.bass as bass
from concourse import mybir

F32 = mybir.dt.float32
F16 = mybir.dt.float16
ALU = mybir.AluOpType
ACT = mybir.ActivationFunctionType
AX = mybir.AxisListType

P = 128
B, S, PATCH, D = 64, 125, 32, 256
HEADS, DK = 4, 64
FF = 1024
DI, NS, DT_RANK = 512, 16, 16
NB = 4
T = NB * S
GROUPS = B // NB
KD, KI, KF = D // P, DI // P, FF // P
Z = PATCH + S
LN_EPS, RMS_EPS = 1e-5, 1e-8
SLOTS = 4
UNITS = 2 * NS
HT = KI // 2
DA_SLOTS, W_SLOTS, BC_SLOTS = 3, 6, 4
POOL_PAIRS = [3, 7, 11]
VECTOR_PAIRS = [q for q in range(NS) if q not in POOL_PAIRS]

PE_PLAN = """
    qk*4 v*2 w_out score*3 w_out skip score turn_p*2 sum w_out turn_p w_out pv turn_p sum pv f1*3 turn_post*2 f1*2
    sum*2 f1 sum f1*2 up*5 sum up*3 sum f2*2 down*4 sumsq f2 sum f2 sum*2 turn_pre*2 sum w_in*8 sum w_x sum w_dt*4
    sum*3
"""
ACT_PLAN = """
    decay*5 softmax*2 decay softmax*2 turn_p*2 decay turn_p pv turn_p decay pv decay f1*3 decay*2 f1*2 decay high
    decay high f1 decay f1 decay f1 gelu square gelu square gelu square gelu square gelu square gelu square gelu
    square gelu square decay*8 store decay*2 turn_pre*2 decay*2 w_in decay w_in*2 silu*2 gate silu gate w_in gate
    silu gate decay*3 w_x decay abs*4 soft_exp soft_log
"""
DVE_PLAN = """
    z*4 qk*2 state read qk*2 v*2 state read maxima*2 add w_out normalise maxima state normalise read maxima state
    read normalise add normalise state read w_out moments_post state read add norm_post state read state read state
    read state low_post read add low_post state read state read add state read state low_gelu*2 read low_gelu add
    low_gelu state read low_gelu*4 state f2 read state read state read add state mean_sq read state read add rms_inv
    down*2 state f2 read moments_pre state read norm_pre add state read state read state read conv*3 state read add
    conv state read state read add state read state read add state read state read add delta du
"""
POOL_PLAN = """
    term*9 root_post term add term*6 square_sum*5 term square_sum*2 term add term*2 rms term*3 root_pre term*3 add
    term*6
"""
SCAN_STAGES = {"skip", "sum", "decay", "state", "read", "add", "term"}
POST_STAGES = {"z", "w_out", "turn_post", "up", "sumsq", "down", "high", "gelu", "square", "store", "moments_post",
               "norm_post", "low_post", "low_gelu", "mean_sq", "rms_inv", "root_post", "square_sum", "rms"}
FREED_BY = dict(w_out="w_out", turn_post="low_post", up="gelu", sumsq="mean_sq", down="down", qk="qk", v="v",
                score="softmax", turn_p="turn_p", pv="pv", f1="f1", f2="f2", turn_pre="turn_pre", w_x="w_x",
                w_dt="abs")
PER_TILE = dict(w_out=2, down=2, f2=2)


def plan(text, scan, post, pre):
    seen = {}
    for word in text.split():
        name, _, times = word.partition("*")
        wanted = scan if name in SCAN_STAGES else post if name in POST_STAGES else pre
        for _ in range(int(times or 1)):
            i = seen[name] = seen.get(name, -1) + 1
            if wanted:
                yield name, i


def ring_tiles(scan, post, pre):
    count, freeing = {"act": 0, "dve": 0}, {}
    for who, text in (("act", ACT_PLAN), ("dve", DVE_PLAN)):
        for name, i in plan(text, scan, post, pre):
            if name in FREED_BY.values() or who == "act" and name in ("w_in", "gate"):
                count[who] += 1
                freeing[name, i] = (who, count[who])
    tile, filled, freed, frees = {}, {}, {}, []
    for name, part in plan(PE_PLAN, scan, post, pre):
        if name in ("skip", "sum"):
            continue
        n = PER_TILE.get(name, 1)
        i = part // n
        if part % n == 0:
            by = FREED_BY.get(name) or ("w_in" if i < KI else "gate")
            tile[name, i] = len(frees)
            freed[name, i] = freeing[by, i - KI if by == "gate" else i]
            frees.append(freed[name, i])
        if part % n == n - 1:
            filled[name, i] = len(filled) + 1
    return tile, filled, freed, frees



def build(nc, ins, out):
    with ExitStack() as ctx:
        def sb(name, shape, dt=F32):
            return ctx.enter_context(nc.sbuf_tensor(name, shape, dt))

        sems = []

        def sem(name):
            s = ctx.enter_context(nc.semaphore(name))
            sems.append(s)
            return s

        ident = sb("ident", [P, P])
        ones = sb("ones", [P, P])
        w_qk = sb("w_qk", [PATCH, 2 * D])
        w_v = sb("w_v", [PATCH, D])
        pos_qk = sb("pos_qk", [P, 4, S])
        pos_v = sb("pos_v", [S, D])
        w_f1 = sb("w_f1", [P, KD, FF])
        b_f1 = sb("b_f1", [P, KF])
        w_f2 = sb("w_f2", [P, KF, D])
        b_f2 = sb("b_f2", [S, D])
        w_in = sb("w_in", [P, KD, 2 * DI])
        w_conv = sb("w_conv", [P, KI, 3])
        w_x = sb("w_x", [P, KI, DT_RANK + 2 * NS])
        w_dt = sb("w_dt", [DT_RANK, DI])
        b_dt = sb("b_dt", [P, KI])
        neg_a = sb("neg_a", [P, KI, NS])
        d_col = sb("d_col", [P, KI])
        d_diag = sb("d_diag", [P, KI, P])
        w_out = sb("w_out", [P, KI, D])
        w_up = sb("w_up", [P, KD, FF], F16)
        w_down = sb("w_down", [P, KF, D], F16)
        half = sb("half", [S, 2 * NB])
        minus_half = sb("minus_half", [S, NB])

        patches = sb("patches", [PATCH, T])
        region_post = sb("region_post", [P, NB * D + KD * T])
        region_pre = sb("region_pre", [P, 2 * KD * T + NB * D + 4 * T])
        region_mlp = sb("region_mlp", [P, KF * T])
        gated = region_post[:, 0:KI * T].rearrange("p (m t) -> p m t", m=KI)
        xn_post = region_post[0:S, 0:NB * D].rearrange("p (b d) -> p b d", b=NB)
        xn_parts = region_post[:, NB * D:NB * D + KD * T].bitcast(F16).rearrange(
            "p (c k t) -> p c k t", c=2, k=KD)
        square = region_post[:, 0:2 * T].rearrange("p (i t) -> p i t", i=2)
        qk = region_pre[:, 0:2 * KD * T].rearrange("p (m t) -> p m t", m=2 * KD)
        xn_t = region_pre[:, 0:KD * T].rearrange("p (k t) -> p k t", k=KD)
        after_qk = region_pre[0:S, 2 * KD * T:2 * KD * T + NB * D + 4 * T]
        v_tok = after_qk[:, 0:NB * D].rearrange("p (b d) -> p b d", b=NB)
        probs = after_qk[:, NB * D:NB * D + 2 * T].rearrange("p (i c t) -> p i c t", i=2, c=4)
        probs_t = after_qk[:, NB * D + 2 * T:NB * D + 4 * T].rearrange("p (i c t) -> p i c t", i=2, c=4)
        relu = region_pre[:, 0:KF * T].rearrange("p (m t) -> p m t", m=KF)
        xn_pre = v_tok
        g_parts = region_mlp[:, :].bitcast(F16).rearrange("p (c m t) -> p c m t", c=2, m=KF)
        padded = region_mlp[:, 0:KI * NB * (S + 2)].rearrange("p (m b t) -> p m b t", m=KI, b=NB)
        soft = region_mlp[:, 0:KI * T].rearrange("p (m t) -> p m t", m=KI)
        linear = region_mlp[:, KI * T:2 * KI * T].rearrange("p (m t) -> p m t", m=KI)
        h1_mem = sb("h1", [P, 2, NB * D])
        h1 = h1_mem[0:S, :, :].rearrange("p c (b d) -> p c b d", b=NB)
        attn_t = h1_mem[:, :, 0:KD * T].rearrange("p c (k t) -> p c k t", k=KD)
        h2 = sb("h2", [S, NB, D])
        u = sb("u", [P, KI, T])
        gate = sb("gate", [P, 2, KI, T])
        delta = sb("delta", [P, KI, T])
        du = sb("du", [P, KI, T])
        x_dbl = sb("x_dbl", [DT_RANK + 2 * NS, T])
        bc = sb("bc", [P, BC_SLOTS, 2, T])
        decay = sb("decay", [P, DA_SLOTS, HT, T])
        work = sb("work", [P, W_SLOTS, HT, T])
        gelu = sb("gelu", [P, 2, T])
        sumsq = sb("sumsq", [P, T])
        row_max = sb("row_max", [S, 4])
        neg_max = sb("neg_max", [S, 2, 4])
        row_sum = sb("row_sum", [S, 2, 4])
        row_inv = sb("row_inv", [S, 4])
        stats = sb("stats", [S, 2, NB, 6])
        mean_var = sb("mean_var", [S, 2, NB, 2])
        var_in = sb("var_in", [S, 2, NB])
        var_pre = sb("var_pre", [S, NB])
        root = sb("root", [S, 2, NB])
        denom = sb("denom", [S, NB])
        norm = sb("norm", [S, NB])
        mean_sq = sb("mean_sq", [S, NB])
        rms = sb("rms", [S, NB])
        rms_eps = sb("rms_eps", [S, NB])
        rms_inv = sb("rms_inv", [S, NB])

        y_acc = [ctx.enter_context(nc.psum_tensor(f"y_acc{m}", [P, 512], F32)) for m in range(KI)]
        ring = [ctx.enter_context(nc.psum_tensor(f"ring{m}", [P, 512], F32)) for m in range(SLOTS)]

        bc_dram = nc.dram_tensor("bc_scratch", [2, 2, NS, T], F32, kind="Internal").ap()

        s_load = sem("s_load")
        s_pe = sem("s_pe")
        s_dve = sem("s_dve")
        s_pool = sem("s_pool")
        s_act = sem("s_act")
        s_tile = sem("s_tile")
        s_tile_act = sem("s_tile_act")
        s_tile_dve = sem("s_tile_dve")
        s_link = sem("s_link")
        s_plink = sem("s_plink")
        s_x = sem("s_x")
        s_bc = [sem(f"s_bc{i}") for i in range(BC_SLOTS)]
        s_bc_out = sem("s_bc_out")
        s_out = sem("s_out")
        s_z = sem("s_z")
        s_skip = sem("s_skip")
        s_decay = sem("s_decay")
        s_term = sem("s_term")
        s_state = sem("s_state")
        s_read = sem("s_read")
        s_pair_dve = sem("s_pair_dve")
        s_pair_pool = sem("s_pair_pool")
        s_sum = sem("s_sum")
        s_var_pre = sem("s_var_pre")
        s_var_post = sem("s_var_post")
        s_root_pre = sem("s_root_pre")
        s_root_post = sem("s_root_post")
        s_xn_pre = sem("s_xn_pre")
        s_xn_post = sem("s_xn_post")
        s_high = sem("s_high")
        s_gelu = sem("s_gelu")
        s_low = sem("s_low")
        s_square = sem("s_square")
        s_sq = sem("s_sq")
        s_ms = sem("s_ms")
        s_rms_inv = sem("s_rms_inv")
        s_nmax = sem("s_nmax")
        s_probs = sem("s_probs")
        s_conv = sem("s_conv")
        s_u = sem("s_u")
        s_abs = sem("s_abs")
        s_log = sem("s_log")
        clear = range(min(s.num for s in sems), max(s.num for s in sems) + 1)
        assert len(clear) == len(sems)

        tmp = [bc[:, :, :, :].rearrange("p a m t -> p (a m t)"), region_pre[:, :],
               gate[:, :, :, :].rearrange("p a m t -> p (a m t)")]

        def scratch(i, lo, n, parts=P):
            return tmp[i][0:parts, lo:lo + n]

        up_raw = work[:, :, :, :].rearrange("p a m t -> p (a m t)")[:, 0:KD * FF]
        down_raw = work[:, :, :, :].rearrange("p a m t -> p (a m t)")[:, 2048:2048 + KF * D]
        below = region_mlp[:, 0:2048]
        f2_nat = scratch(0, 0, KD * FF).rearrange("p (k f) -> p k f", k=KD)
        f2_t = scratch(1, 0, KF * D).rearrange("p (k f) -> p k f", k=KF)
        proj = scratch(2, 0, 1024).rearrange("p (k f) -> p k f", k=KD)
        proj_v = scratch(2, 1024, 512).rearrange("p (k f) -> p k f", k=KD)
        hw1 = scratch(2, 1536, 256).rearrange("p (k f) -> p k f", k=KD)
        fw1 = scratch(2, 1792, 256)
        hw2 = scratch(2, 2048, 256).rearrange("p (k f) -> p k f", k=KD)
        fw2 = scratch(2, 2304, 256)
        emb = scratch(2, 2560, KD * Z).rearrange("p (k z) -> p k z", k=KD)
        emb2 = scratch(2, 2900, KD * Z).rearrange("p (k z) -> p k z", k=KD)
        hid1 = scratch(2, 3240, Z)
        c1_rep = scratch(2, 3400, P)
        cols = scratch(2, 3540, 16)
        small = scratch(2, 3560, 16)
        rows = scratch(0, 2100, 768, 1)
        hid2 = region_post[:, 0:FF]

        loads = [
            (ident[:, :], "ident"), (emb[:, :, :], "emb"), (cols, "cols"), (hw1, "hw1"), (fw1, "fw1"),
            (proj, "proj"), (proj_v, "proj_v"), (rows, "rows"), (hw2, "hw2"), (fw2, "fw2"), (f2_nat, "f2_nat"),
            (f2_t, "f2_t"), (up_raw, "up"), (down_raw, "down"), (neg_a[:, :, :], "a_log"), (d_col[:, :], "d_col"),
            (w_f1[:, :, :], "f1"), (b_f1[:, :], "f1b"), (w_in[:, :, :], "w_in"), (w_conv[:, :, :], "w_conv"),
            (w_x[:, :, :], "w_x"), (w_dt[:, :], "w_dt"), (b_dt[:, :], "b_dt"), (w_out[:, :, :], "w_out"),
        ]
        with nc.Block() as block:
            @block.sync
            def _(sp):
                for dst, name in loads:
                    sp.dma_start(dst, ins[name]).then_inc(s_load, 16)
                sp.wait_ge(s_load, 16 * len(loads))

            @block.gpsimd
            def _(pool):
                nc.gpsimd.memset(decay[:, :, :, :], 0.0).then_inc(s_pool, 1)

            @block.scalar
            def _(act):
                act.wait_ge(s_load, 16 * len(loads))
                nc.scalar.activation(neg_a[:, :, :], neg_a[:, :, :], ACT.Exp).then_inc(s_act, 1)

            @block.tensor
            def _(pe):
                pe.wait_ge(s_load, 16 * len(loads))
                pe.wait_ge(s_dve, 2)
                for k in range(KD):
                    mm = nc.tensor.matmul(ring[0][:, 0:Z], hw1[:, k, :], emb[:, k, :], start=(k == 0),
                                          stop=(k == KD - 1))
                mm.then_inc(s_pe, 1)
                for k in range(KD):
                    for h in range(2):
                        mm = nc.tensor.matmul(ring[2 + h][:, :], hw2[:, k, :], f2_nat[:, k, h * 512:(h + 1) * 512],
                                              start=(k == 0), stop=(k == KD - 1))
                for k in range(KD):
                    mm = nc.tensor.matmul(y_acc[0][:, 0:1], hw2[:, k, :], cols[:, 10 + k:11 + k], start=(k == 0),
                                          stop=(k == KD - 1))
                mm.then_inc(s_pe, 1)
                for i in range(2):
                    pe.wait_ge(s_dve, 3 + i)
                    mm = nc.tensor.matmul(y_acc[1 + i][:, 0:1], ones[:, :], small[:, 1 + i:2 + i], start=True,
                                          stop=True)
                mm.then_inc(s_pe, 1)
                pe.wait_ge(s_dve, 5)
                for m in range(KD):
                    mm = nc.tensor.matmul(ring[m][:, 0:Z], fw1[:, m * P:(m + 1) * P], hid1, start=True, stop=True)
                mm.then_inc(s_pe, 1)
                pe.wait_ge(s_dve, 6)
                for m in range(4):
                    for k in range(KD):
                        mm = nc.tensor.matmul(ring[0][:, m * S:(m + 1) * S], proj[:, k, m * P:(m + 1) * P],
                                              emb2[:, k, PATCH:Z], start=(k == 0), stop=(k == KD - 1))
                for k in range(KD):
                    mm = nc.tensor.matmul(ring[1][0:PATCH, :], emb2[:, k, 0:PATCH], proj[:, k, :], start=(k == 0),
                                          stop=(k == KD - 1))
                mm.then_inc(s_pe, 1)
                pe.wait_ge(s_dve, 8)
                for k in range(KD):
                    mm = nc.tensor.matmul(y_acc[0][0:PATCH, 0:D], emb2[:, k, 0:PATCH], proj_v[:, k, :],
                                          start=(k == 0), stop=(k == KD - 1))
                for k in range(KD):
                    nc.tensor.matmul(y_acc[1][0:S, 0:D], emb2[:, k, PATCH:Z], proj_v[:, k, :], start=(k == 0),
                                     stop=False)
                nc.tensor.matmul(y_acc[1][0:S, 0:D], ones[0:1, 0:S], rows[0:1, 0:D], start=False, stop=True)
                nc.tensor.matmul(y_acc[2][0:S, 0:D], c1_rep[:, 0:S], fw2, start=True, stop=False)
                nc.tensor.matmul(y_acc[2][0:S, 0:D], ones[0:1, 0:S], rows[0:1, D:2 * D], start=False, stop=False)
                mm = nc.tensor.matmul(y_acc[2][0:S, 0:D], ones[0:1, 0:S], rows[0:1, 2 * D:3 * D], start=False,
                                      stop=True)
                mm.then_inc(s_pe, 1)
                for f in range(KF):
                    if f >= 2:
                        pe.wait_ge(s_dve, 8 + f - 1)
                    nc.tensor.matmul(ring[2 + f % 2][:, 0:D], hid2[:, f * P:(f + 1) * P], fw2, start=True,
                                     stop=True).then_inc(s_pe, 1)

            @block.vector
            def _(dve):
                linked = [0]

                def link(ins_):
                    linked[0] += 1
                    ins_.then_inc(s_link, 1)
                    dve.wait_ge(s_link, linked[0])

                nc.vector.memset(ones[:, :], 1.0)
                nc.vector.memset(half[:, :], 0.5)
                nc.vector.memset(minus_half[:, :], -0.5).then_inc(s_dve, 1)
                dve.wait_ge(s_load, 16 * len(loads))
                for k in range(KD):
                    ins_ = nc.vector.tensor_scalar(emb[:, k, PATCH:Z], emb[:, k, PATCH:Z], cols[:, k:k + 1], None,
                                                   ALU.add)
                ins_.then_inc(s_dve, 1)
                for i, w in enumerate((up_raw, down_raw)):
                    nc.vector.tensor_reduce(small[:, 1 + i:2 + i], w, AX.X, ALU.add,
                                            apply_absolute_value=True).then_inc(s_dve, 1)
                dve.wait_ge(s_pe, 1)
                nc.vector.tensor_copy(hid1[:, 0:PATCH], ring[0][:, 0:PATCH])
                nc.vector.tensor_scalar(hid1[:, PATCH:Z], ring[0][:, PATCH:Z], cols[:, 2:3], None,
                                        ALU.add).then_inc(s_dve, 1)
                dve.wait_ge(s_pe, 4)
                for m in range(KD):
                    link(nc.vector.tensor_tensor(emb2[:, m, :], ring[m][:, 0:Z], emb[:, m, :], ALU.add))
                    ins_ = nc.vector.tensor_scalar(emb2[:, m, PATCH:Z], emb2[:, m, PATCH:Z], cols[:, 3 + m:4 + m],
                                                   None, ALU.add)
                ins_.then_inc(s_dve, 1)
                nc.vector.tensor_copy(hid2[:, 0:512], ring[2][:, :])
                nc.vector.tensor_copy(hid2[:, 512:1024], ring[3][:, :]).then_inc(s_dve, 1)
                link(nc.vector.tensor_scalar(small[:, 0:1], y_acc[0][:, 0:1], cols[:, 9:10], None, ALU.add))
                nc.vector.tensor_scalar(c1_rep, ones[:, :], small[:, 0:1], None, ALU.mult)
                for i in range(2):
                    nc.vector.tensor_scalar(small[:, 3 + i:4 + i], y_acc[1 + i][:, 0:1], 0.5 / (D * FF), None, ALU.mult)
                    ins_ = nc.vector.tensor_scalar(small[:, 5 + i:6 + i], y_acc[1 + i][:, 0:1], -0.5 / (D * FF), None,
                                                   ALU.mult)
                ins_.then_inc(s_dve, 1)
                dve.wait_ge(s_dve, 8)
                for f in range(KF):
                    dve.wait_ge(s_pe, 7 + f)
                    nc.vector.tensor_tensor(w_f2[:, f, :], ring[2 + f % 2][:, 0:D], f2_t[:, f, :],
                                            ALU.add).then_inc(s_dve, 1)
                for i, (w, dst) in enumerate(((up_raw, w_up), (down_raw, w_down))):
                    flat = dst[:, :, :].rearrange("p a b -> p (a b)")
                    link(nc.vector.tensor_scalar(below, w, small[:, 5 + i:6 + i], None, ALU.is_lt))
                    link(nc.vector.scalar_tensor_tensor(out=flat, in0=w, scalar=small[:, 3 + i:4 + i], in1=below,
                                                        op0=ALU.is_gt, op1=ALU.subtract))
                for m in range(4):
                    nc.vector.tensor_scalar(pos_qk[:, m, :], ring[0][:, m * S:(m + 1) * S], cols[:, 5 + m:6 + m], None,
                                            ALU.add)
                nc.vector.tensor_copy(w_qk[:, :], ring[1][0:PATCH, :])
                nc.vector.tensor_copy(w_v[:, :], y_acc[0][0:PATCH, 0:D])
                nc.vector.tensor_copy(pos_v[:, :], y_acc[1][0:S, 0:D])
                nc.vector.tensor_copy(b_f2[:, :], y_acc[2][0:S, 0:D])
                for m in range(KI):
                    nc.vector.tensor_scalar(d_diag[:, m, :], ident[:, :], d_col[:, m:m + 1], None, ALU.mult)
                dve.wait_ge(s_act, 1)
                link(nc.vector.tensor_scalar(neg_a[:, :, :], neg_a[:, :, :], -1.0, None, ALU.mult))
        nc.all_engine_barrier(sems_to_clear=clear)

        def step(c, scan, post, pre, x_cols=None, out_rows=None):
            o = 1 - c
            tile, filled, freed, frees = ring_tiles(scan, post, pre)
            pair_of = [(j // 4, (j // 2) % 2, 2 * (j // 4) + j % 2) for j in range(UNITS)]

            def last_unit(n):
                return 4 * (n // 2) + 2 + n % 2

            def wait_freed(eng, name, i):
                who, n = freed[name, i]
                eng.wait_ge(s_tile_act if who == "act" else s_tile_dve, n)

            def wait_tile(eng, name, i):
                eng.wait_ge(s_tile, filled[name, i])

            def bank(name, i):
                return ring[tile[name, i] % SLOTS]

            def wait_bank(eng, name, i):
                t = tile[name, i]
                if t >= SLOTS:
                    who, n = frees[t - SLOTS]
                    eng.wait_ge(s_tile_act if who == "act" else s_tile_dve, n)

            with nc.Block() as block:
                @block.sync
                def _(sp):
                    if pre:
                        sp.dma_start(patches[:, :], x_cols).then_inc(s_x, 16)
                    if scan:
                        for n in range(NS):
                            if n >= BC_SLOTS:
                                sp.wait_ge(s_read, last_unit(n - BC_SLOTS) + 1)
                                sp.wait_ge(s_term, last_unit(n - BC_SLOTS) + 1)
                            src = bc_dram[c, :, n, :].unsqueeze(0).to_broadcast([P, 2, T])
                            sp.dma_start(bc[:, n % BC_SLOTS], src).then_inc(s_bc[n % BC_SLOTS], 16)
                    if pre:
                        wait_freed(sp, "w_x", 0)
                        sp.dma_start(bc_dram[o].rearrange("i n t -> (i n) t"),
                                     x_dbl[DT_RANK:DT_RANK + 2 * NS, :]).then_inc(s_bc_out, 16)
                        sp.wait_ge(s_bc_out, 16)
                        sp.wait_ge(s_x, 16)
                    if post:
                        sp.wait_ge(s_out, 16)

                @block.gpsimd
                def _(pool):
                    def term(j):
                        p, h, n = pair_of[j]
                        pool.wait_ge(s_bc[n % BC_SLOTS], 16 * (n // BC_SLOTS + 1))
                        if j >= W_SLOTS:
                            pool.wait_ge(s_sum, (j - W_SLOTS) // 2 + 1)
                        nc.gpsimd.tensor_tensor(
                            work[:, j % W_SLOTS], du[:, HT * h:HT * h + HT, :],
                            bc[:, n % BC_SLOTS, 0].unsqueeze(1).to_broadcast([P, HT, T]),
                            ALU.mult).then_inc(s_term, 1)

                    def add(i):
                        q = POOL_PAIRS[i]
                        pool.wait_ge(s_read, 2 * q + 2)
                        first = work[:, 2 * q % W_SLOTS]
                        nc.gpsimd.tensor_tensor(first, first, work[:, (2 * q + 1) % W_SLOTS],
                                                ALU.add).then_inc(s_pair_pool, 1)

                    def root_post(i):
                        pool.wait_ge(s_var_post, 1)
                        nc.gpsimd.tensor_tensor(root[:, :, :], var_in[:, :, :],
                                                half[:, :].rearrange("p (a b) -> p a b", a=2),
                                                ALU.pow).then_inc(s_root_post, 1)

                    def root_pre(i):
                        pool.wait_ge(s_var_pre, 1)
                        nc.gpsimd.tensor_tensor(norm[:, :], var_pre[:, :], minus_half[:, :],
                                                ALU.pow).then_inc(s_root_pre, 1)

                    def square_sum(i):
                        m = i + 1
                        pool.wait_ge(s_square, m + 1)
                        if m >= 2:
                            pool.wait_ge(s_sq, m - 1)
                        nc.gpsimd.tensor_tensor(sumsq[:, :], sumsq[:, :], square[:, m % 2], ALU.add).then_inc(s_sq, 1)

                    def rms_(i):
                        wait_freed(pool, "sumsq", 0)
                        nc.gpsimd.tensor_tensor(rms[:, :], mean_sq[:, :], half[:, 0:NB], ALU.pow).then_inc(s_ms, 1)

                    stages = dict(term=term, add=add, root_post=root_post, root_pre=root_pre, square_sum=square_sum,
                                  rms=rms_)
                    for name, i in plan(POOL_PLAN, scan, post, pre):
                        stages[name](i)

                @block.scalar
                def _(act):
                    def decays(j):
                        p, h, n = pair_of[j]
                        if j >= DA_SLOTS:
                            act.wait_ge(s_state, j - DA_SLOTS + 1)
                        for m in range(HT):
                            dst = decay[:, j % DA_SLOTS, m].rearrange("p (b t) -> p b t", b=NB)[:, :, 1:S]
                            src = delta[:, HT * h + m].rearrange("p (b t) -> p b t", b=NB)[:, :, 1:S]
                            ins_ = nc.scalar.activation(dst, src, ACT.Exp, scale=neg_a[:, HT * h + m, n:n + 1])
                        ins_.then_inc(s_decay, 1)

                    def high(k):
                        wait_tile(act, "turn_post", k)
                        nc.scalar.activation(xn_parts[:, 0, k], bank("turn_post", k)[:, 0:T],
                                             ACT.Copy).then_inc(s_high, 1)

                    def gelu_(m):
                        wait_tile(act, "up", m)
                        if m >= 2:
                            act.wait_ge(s_low, m - 1)
                            act.wait_ge(s_square, m - 1)
                        nc.scalar.activation(g_parts[:, 0, m], bank("up", m)[:, 0:T], ACT.Gelu).then_inc(s_gelu, 1)
                        nc.scalar.activation(gelu[:, m % 2], bank("up", m)[:, 0:T], ACT.Gelu).then_inc(s_tile_act, 1)

                    def square_(m):
                        wait_freed(act, "up", m)
                        if m >= 3:
                            act.wait_ge(s_sq, m - 2)
                        dst = square[:, m % 2] if m else sumsq[:, :]
                        nc.scalar.activation(dst, gelu[:, m % 2], ACT.Square).then_inc(s_square, 1)

                    def store(i):
                        wait_freed(act, "down", 1)
                        act.dma_start(out_rows, h2[:, :, :]).then_inc(s_out, 16)

                    def softmax(i):
                        wait_tile(act, "score", i)
                        act.wait_ge(s_nmax, i + 1)
                        if i >= 2:
                            wait_tile(act, "turn_p", i - 2)
                            act.wait_ge(s_probs, i - 1)
                        for q in range(4):
                            ins_ = nc.scalar.activation(probs[:, i % 2, q], bank("score", i)[0:S, q * S:(q + 1) * S],
                                                        ACT.Exp, bias=neg_max[:, i % 2, q:q + 1], scale=DK ** -0.5,
                                                        accum_out=row_sum[:, i % 2, q:q + 1])
                        ins_.then_inc(s_tile_act, 1)

                    def turn_p(i):
                        wait_tile(act, "turn_p", i)
                        if i >= 2:
                            wait_tile(act, "pv", i // 2 - 1)
                        nc.scalar.activation(probs_t[:, i % 2].rearrange("p c t -> p (c t)"),
                                             bank("turn_p", i)[0:S, 0:T], ACT.Copy).then_inc(s_tile_act, 1)

                    def pv(i):
                        wait_tile(act, "pv", i)
                        if post:
                            wait_freed(act, "w_out", 1)
                        nc.scalar.activation(attn_t[:, o, :, 2 * S * i:2 * S * (i + 1)],
                                             bank("pv", i)[:, 0:T].rearrange("p (k t) -> p k t", k=KD),
                                             ACT.Copy).then_inc(s_tile_act, 1)

                    def f1(m):
                        wait_tile(act, "f1", m)
                        nc.scalar.activation(relu[:, m], bank("f1", m)[:, 0:T], ACT.Relu,
                                             bias=b_f1[:, m:m + 1]).then_inc(s_tile_act, 1)

                    def turn_pre(k):
                        wait_tile(act, "turn_pre", k)
                        nc.scalar.activation(xn_t[:, k], bank("turn_pre", k)[:, 0:T], ACT.Copy).then_inc(s_tile_act, 1)

                    def w_in_(m):
                        wait_tile(act, "w_in", m)
                        nc.scalar.activation(padded[:, m, :, 2:S + 2],
                                             bank("w_in", m)[:, 0:T].rearrange("p (b t) -> p b t", b=NB), ACT.Copy)
                        if scan and m == 0:
                            act.wait_ge(s_skip, 1)
                        nc.scalar.activation(u[:, m], bank("w_in", m)[:, 0:T], ACT.Identity,
                                             scale=w_conv[:, m, 2:3]).then_inc(s_tile_act, 1)

                    def gate_(m):
                        wait_tile(act, "w_in", KI + m)
                        if post:
                            act.wait_ge(s_z, KI)
                        nc.scalar.activation(gate[:, o, m], bank("w_in", KI + m)[:, 0:T],
                                             ACT.Silu).then_inc(s_tile_act, 1)

                    def silu(m):
                        act.wait_ge(s_conv, m + 1)
                        nc.scalar.activation(u[:, m], u[:, m], ACT.Silu).then_inc(s_u, 1)

                    def w_x_(i):
                        wait_tile(act, "w_x", 0)
                        nc.scalar.activation(x_dbl[:, :], bank("w_x", 0)[0:DT_RANK + 2 * NS, 0:T],
                                             ACT.Copy).then_inc(s_tile_act, 1)

                    def absolute(m):
                        wait_tile(act, "w_dt", m)
                        act.wait_ge(s_conv, KI)
                        nc.scalar.activation(soft[:, m], bank("w_dt", m)[:, 0:T], ACT.Abs,
                                             bias=b_dt[:, m:m + 1]).then_inc(s_abs, 1)
                        nc.scalar.activation(linear[:, m], bank("w_dt", m)[:, 0:T], ACT.Relu,
                                             bias=b_dt[:, m:m + 1]).then_inc(s_tile_act, 1)

                    def soft_exp(i):
                        act.wait_ge(s_abs, KI)
                        nc.scalar.activation(soft, soft, ACT.Exp, scale=-1.0).then_inc(s_abs, 1)

                    def soft_log(i):
                        act.wait_ge(s_abs, KI + 1)
                        nc.scalar.activation(soft, soft, ACT.Ln, bias=1.0).then_inc(s_log, 1)

                    stages = dict(decay=decays, high=high, gelu=gelu_, square=square_, store=store, softmax=softmax,
                                  turn_p=turn_p, pv=pv, f1=f1, turn_pre=turn_pre, w_in=w_in_, gate=gate_, silu=silu,
                                  w_x=w_x_, abs=absolute, soft_exp=soft_exp, soft_log=soft_log)
                    for name, i in plan(ACT_PLAN, scan, post, pre):
                        stages[name](i)

                @block.tensor
                def _(pe):
                    def skip(i):
                        for m in range(KI):
                            if post:
                                pe.wait_ge(s_z, m + 1)
                            ins_ = nc.tensor.matmul(y_acc[m][:, 0:T], d_diag[:, m, :], u[:, m], start=True,
                                                    stop=False, skip_group_check=True)
                        ins_.then_inc(s_skip, 1)

                    def sum_pair(q):
                        if q in POOL_PAIRS:
                            pe.wait_ge(s_pair_pool, POOL_PAIRS.index(q) + 1)
                        else:
                            pe.wait_ge(s_pair_dve, VECTOR_PAIRS.index(q) + 1)
                        for m in range(HT):
                            ins_ = nc.tensor.matmul(y_acc[HT * (q % 2) + m][:, 0:T], ident[:, :],
                                                    work[:, (2 * q) % W_SLOTS, m], start=False, stop=(q >= NS - 2),
                                                    skip_group_check=True)
                        ins_.then_inc(s_sum, 1)

                    def w_out_(i):
                        if i == 0:
                            pe.wait_ge(s_z, KI)
                        if i % 2 == 0:
                            wait_bank(pe, "w_out", i // 2)
                        for k in range(KI):
                            mm = nc.tensor.matmul(bank("w_out", i // 2)[0:S, (i % 2) * D:(i % 2 + 1) * D],
                                                  gated[:, k, i * S:(i + 1) * S], w_out[:, k, :], start=(k == 0),
                                                  stop=(k == KI - 1))
                        if i % 2:
                            mm.then_inc(s_tile, 1)

                    def turn(name, k, xn):
                        wait_bank(pe, name, k)
                        for b in range(NB):
                            mm = nc.tensor.transpose(bank(name, k)[:, b * S:(b + 1) * S],
                                                     xn[:, b, k * P:(k + 1) * P], ident[0:S, 0:S])
                        mm.then_inc(s_tile, 1)

                    def turn_post(k):
                        pe.wait_ge(s_xn_post, NB)
                        turn("turn_post", k, xn_post)

                    def turn_pre(k):
                        pe.wait_ge(s_xn_pre, NB)
                        turn("turn_pre", k, xn_pre)

                    def up(m):
                        wait_freed(pe, "turn_post", 1)
                        wait_bank(pe, "up", m)
                        for k in range(KD):
                            for part in range(2):
                                mm = nc.tensor.matmul(bank("up", m)[:, 0:T], w_up[:, k, m * P:(m + 1) * P],
                                                      xn_parts[:, part, k], start=(k == 0 and part == 0),
                                                      stop=(k == KD - 1 and part == 1))
                        mm.then_inc(s_tile, 1)

                    def sumsq_(i):
                        pe.wait_ge(s_sq, KF - 1)
                        wait_bank(pe, "sumsq", 0)
                        for b in range(NB):
                            mm = nc.tensor.matmul(bank("sumsq", 0)[0:S, b:b + 1], sumsq[:, b * S:(b + 1) * S],
                                                  ones[:, 0:1], start=True, stop=True)
                        mm.then_inc(s_tile, 1)

                    def down(i):
                        if i == 0:
                            pe.wait_ge(s_low, KF)
                        if i % 2 == 0:
                            wait_bank(pe, "down", i // 2)
                        for m in range(KF):
                            for part in range(2):
                                mm = nc.tensor.matmul(bank("down", i // 2)[0:S, (i % 2) * D:(i % 2 + 1) * D],
                                                      g_parts[:, part, m, i * S:(i + 1) * S], w_down[:, m, :],
                                                      start=(m == 0 and part == 0),
                                                      stop=(m == KF - 1 and part == 1))
                        if i % 2:
                            mm.then_inc(s_tile, 1)

                    def qk_(m):
                        pe.wait_ge(s_x, 16)
                        wait_bank(pe, "qk", m)
                        nc.tensor.matmul(bank("qk", m)[:, 0:T], w_qk[:, m * P:(m + 1) * P], patches[:, :], start=True,
                                         stop=True).then_inc(s_tile, 1)

                    def v_(i):
                        pe.wait_ge(s_x, 16)
                        wait_bank(pe, "v", i)
                        for b in range(2):
                            t0 = (2 * i + b) * S
                            mm = nc.tensor.matmul(bank("v", i)[0:S, b * D:(b + 1) * D], patches[:, t0:t0 + S],
                                                  w_v[:, :], start=True, stop=True)
                        mm.then_inc(s_tile, 1)

                    def score(i):
                        wait_freed(pe, "qk", 2 * KD - 1)
                        wait_bank(pe, "score", i)
                        r = DK * (i % 2)
                        for hh in range(2):
                            for b in range(2):
                                t0 = (2 * (i // 2) + b) * S
                                q = 2 * hh + b
                                mm = nc.tensor.matmul(bank("score", i)[0:S, q * S:(q + 1) * S],
                                                      qk[r:r + DK, hh, t0:t0 + S], qk[r:r + DK, 2 + hh, t0:t0 + S],
                                                      start=True, stop=True)
                        mm.then_inc(s_tile, 1)

                    def turn_p(i):
                        pe.wait_ge(s_probs, i + 1)
                        wait_bank(pe, "turn_p", i)
                        for q in range(4):
                            mm = nc.tensor.transpose(bank("turn_p", i)[0:S, q * S:(q + 1) * S], probs[:, i % 2, q],
                                                     ident[0:S, 0:S])
                        mm.then_inc(s_tile, 1)

                    def pv(i):
                        wait_freed(pe, "turn_p", 2 * i + 1)
                        wait_freed(pe, "v", 1)
                        wait_bank(pe, "pv", i)
                        for odd in range(2):
                            for hh in range(2):
                                for b in range(2):
                                    q = 2 * hh + b
                                    h0 = (2 * hh + odd) * DK
                                    mm = nc.tensor.matmul(bank("pv", i)[DK * odd:DK * (odd + 1), q * S:(q + 1) * S],
                                                          v_tok[:, 2 * i + b, h0:h0 + DK], probs_t[:, odd, q],
                                                          start=True, stop=True)
                        mm.then_inc(s_tile, 1)

                    def f1(m):
                        wait_freed(pe, "pv", 1)
                        wait_bank(pe, "f1", m)
                        for k in range(KD):
                            mm = nc.tensor.matmul(bank("f1", m)[:, 0:T], w_f1[:, k, m * P:(m + 1) * P], attn_t[:, o, k],
                                                  start=(k == 0), stop=(k == KD - 1))
                        mm.then_inc(s_tile, 1)

                    def f2(i):
                        if i == 0:
                            wait_freed(pe, "f1", KF - 1)
                        if i % 2 == 0:
                            wait_bank(pe, "f2", i // 2)
                        for m in range(KF):
                            mm = nc.tensor.matmul(bank("f2", i // 2)[0:S, (i % 2) * D:(i % 2 + 1) * D],
                                                  relu[:, m, i * S:(i + 1) * S], w_f2[:, m, :], start=(m == 0),
                                                  stop=(m == KF - 1))
                        if i % 2:
                            mm.then_inc(s_tile, 1)

                    def w_in_(m):
                        wait_freed(pe, "turn_pre", 1)
                        wait_bank(pe, "w_in", m)
                        for k in range(KD):
                            mm = nc.tensor.matmul(bank("w_in", m)[:, 0:T], w_in[:, k, m * P:(m + 1) * P], xn_t[:, k],
                                                  start=(k == 0), stop=(k == KD - 1))
                        mm.then_inc(s_tile, 1)

                    def w_x_(i):
                        pe.wait_ge(s_u, KI)
                        wait_bank(pe, "w_x", 0)
                        for k in range(KI):
                            mm = nc.tensor.matmul(bank("w_x", 0)[0:DT_RANK + 2 * NS, 0:T], w_x[:, k, :], u[:, k],
                                                  start=(k == 0), stop=(k == KI - 1))
                        mm.then_inc(s_tile, 1)

                    def w_dt_(m):
                        wait_freed(pe, "w_x", 0)
                        wait_bank(pe, "w_dt", m)
                        nc.tensor.matmul(bank("w_dt", m)[:, 0:T], w_dt[:, m * P:(m + 1) * P], x_dbl[0:DT_RANK, :],
                                         start=True, stop=True).then_inc(s_tile, 1)

                    stages = dict(skip=skip, sum=sum_pair, w_out=w_out_, turn_post=turn_post, up=up, sumsq=sumsq_,
                                  down=down, qk=qk_, v=v_, score=score, turn_p=turn_p, pv=pv, f1=f1, f2=f2,
                                  turn_pre=turn_pre, w_in=w_in_, w_x=w_x_, w_dt=w_dt_)
                    for name, i in plan(PE_PLAN, scan, post, pre):
                        stages[name](i)

                @block.vector
                def _(dve):
                    linked = [0]

                    def link(ins_):
                        linked[0] += 1
                        ins_.then_inc(s_link, 1)
                        dve.wait_ge(s_link, linked[0])

                    def state(j):
                        dve.wait_ge(s_decay, j + 1)
                        dve.wait_ge(s_term, j + 1)
                        w = work[:, j % W_SLOTS].rearrange("p m t -> p (m t)")
                        nc.vector.tensor_tensor_scan(w, decay[:, j % DA_SLOTS].rearrange("p m t -> p (m t)"), w, 0.0,
                                                     ALU.mult, ALU.add).then_inc(s_state, 1)

                    def read(j):
                        p, h, n = pair_of[j]
                        dve.wait_ge(s_state, j + 1)
                        w = work[:, j % W_SLOTS]
                        nc.vector.tensor_tensor(w, w, bc[:, n % BC_SLOTS, 1].unsqueeze(1).to_broadcast([P, HT, T]),
                                                ALU.mult).then_inc(s_read, 1)

                    def add(i):
                        q = VECTOR_PAIRS[i]
                        dve.wait_ge(s_read, 2 * q + 2)
                        first = work[:, 2 * q % W_SLOTS]
                        nc.vector.tensor_tensor(first, first, work[:, (2 * q + 1) % W_SLOTS],
                                                ALU.add).then_inc(s_pair_dve, 1)

                    def z(m):
                        nc.vector.tensor_tensor(gated[:, m], y_acc[m][:, 0:T], gate[:, o, m],
                                                ALU.mult).then_inc(s_z, 1)

                    def w_out_(i):
                        wait_tile(dve, "w_out", i)
                        nc.vector.tensor_tensor(h2[:, 2 * i:2 * i + 2, :],
                                                bank("w_out", i)[0:S, :].rearrange("p (b d) -> p b d", b=2),
                                                h1[:, o, 2 * i:2 * i + 2, :], ALU.add).then_inc(s_tile_dve, 1)

                    def moments(h, i):
                        for b in range(NB):
                            ins_ = nc.vector.bn_stats(stats[:, i, b, :], h[:, b, :])
                        link(ins_)
                        for b in range(NB):
                            ins_ = nc.vector.bn_aggr(mean_var[:, i, b, :], stats[:, i, b, :])
                        link(ins_)

                    def normed(xn, h, i, scale, ready):
                        for b in range(NB):
                            nc.vector.tensor_scalar(xn[:, b, :], h[:, b, :], mean_var[:, i, b, 0:1], scale[:, b:b + 1],
                                                    ALU.subtract, ALU.mult).then_inc(ready, 1)

                    def moments_post(i):
                        wait_freed(dve, "w_out", 1)
                        moments(h2, 1)
                        nc.vector.tensor_copy(var_in[:, 0, :], mean_var[:, 1, :, 1])
                        nc.vector.tensor_scalar(var_in[:, 1, :], mean_var[:, 1, :, 1], LN_EPS, None,
                                                ALU.add).then_inc(s_var_post, 1)

                    def norm_post(i):
                        dve.wait_ge(s_root_post, 1)
                        link(nc.vector.scalar_tensor_tensor(out=denom[:, :], in0=root[:, 1, :], scalar=RMS_EPS,
                                                            in1=root[:, 0, :], op0=ALU.mult, op1=ALU.add))
                        link(nc.vector.reciprocal(denom[:, :], denom[:, :]))
                        normed(xn_post, h2, 1, denom, s_xn_post)

                    def moments_pre(i):
                        wait_freed(dve, "f2", 1)
                        moments(h1[:, o], 0)
                        nc.vector.tensor_scalar(var_pre[:, :], mean_var[:, 0, :, 1], LN_EPS, None,
                                                ALU.add).then_inc(s_var_pre, 1)
                        if post:
                            wait_tile(dve, "down", 1)
                        nc.vector.memset(padded[:, :, :, 0:2], 0.0)

                    def norm_pre(i):
                        dve.wait_ge(s_root_pre, 1)
                        normed(xn_pre, h1[:, o], 0, norm, s_xn_pre)

                    def low_post(k):
                        dve.wait_ge(s_high, k + 1)
                        nc.vector.tensor_tensor(xn_parts[:, 1, k], bank("turn_post", k)[:, 0:T], xn_parts[:, 0, k],
                                                ALU.subtract).then_inc(s_tile_dve, 1)

                    def low_gelu(m):
                        wait_freed(dve, "up", m)
                        nc.vector.tensor_tensor(g_parts[:, 1, m], gelu[:, m % 2], g_parts[:, 0, m],
                                                ALU.subtract).then_inc(s_low, 1)

                    def mean_sq_(i):
                        wait_tile(dve, "sumsq", 0)
                        nc.vector.tensor_scalar(mean_sq[:, :], bank("sumsq", 0)[0:S, 0:NB], 1.0 / FF, None,
                                                ALU.mult).then_inc(s_tile_dve, 1)

                    def rms_inv_(i):
                        dve.wait_ge(s_ms, 1)
                        link(nc.vector.tensor_scalar(rms_eps[:, :], rms[:, :], RMS_EPS, None, ALU.add))
                        nc.vector.reciprocal(rms_inv[:, :], rms_eps[:, :]).then_inc(s_rms_inv, 1)

                    def down(i):
                        dve.wait_ge(s_rms_inv, 1)
                        wait_tile(dve, "down", i)
                        for b in range(2):
                            s = 2 * i + b
                            ins_ = nc.vector.scalar_tensor_tensor(
                                out=h2[:, s, :], in0=bank("down", i)[0:S, b * D:(b + 1) * D],
                                scalar=rms_inv[:, s:s + 1], in1=h2[:, s, :], op0=ALU.mult, op1=ALU.add)
                        ins_.then_inc(s_tile_dve, 1)

                    def qk_(m):
                        wait_tile(dve, "qk", m)
                        nc.vector.tensor_tensor(
                            qk[:, m].rearrange("p (b t) -> p b t", b=NB),
                            bank("qk", m)[:, 0:T].rearrange("p (b t) -> p b t", b=NB),
                            pos_qk[:, m].unsqueeze(1).to_broadcast([P, NB, S]), ALU.add).then_inc(s_tile_dve, 1)

                    def v_(i):
                        wait_tile(dve, "v", i)
                        nc.vector.tensor_tensor(
                            v_tok[:, 2 * i:2 * i + 2, :], bank("v", i)[0:S, :].rearrange("p (b d) -> p b d", b=2),
                            pos_v[:, :].unsqueeze(1).to_broadcast([S, 2, D]), ALU.add).then_inc(s_tile_dve, 1)

                    def maxima(i):
                        wait_tile(dve, "score", i)
                        if i >= 2:
                            wait_freed(dve, "score", i - 2)
                        if i >= 1:
                            dve.wait_ge(s_nmax, i)
                        link(nc.vector.tensor_reduce(row_max[:, :],
                                                     bank("score", i)[0:S, 0:T].rearrange("p (q t) -> p q t", q=4),
                                                     AX.X, ALU.max))
                        nc.vector.tensor_scalar(neg_max[:, i % 2, :], row_max[:, :], -DK ** -0.5, None,
                                                ALU.mult).then_inc(s_nmax, 1)

                    def normalise(i):
                        wait_freed(dve, "score", i)
                        if i >= 1:
                            dve.wait_ge(s_probs, i)
                        link(nc.vector.reciprocal(row_inv[:, :], row_sum[:, i % 2, :]))
                        nc.vector.tensor_tensor(probs[:, i % 2], probs[:, i % 2],
                                                row_inv[:, :].unsqueeze(2).to_broadcast([S, 4, S]),
                                                ALU.mult).then_inc(s_probs, 1)

                    def f2(i):
                        wait_tile(dve, "f2", i)
                        nc.vector.tensor_tensor(h1[:, o, 2 * i:2 * i + 2, :],
                                                bank("f2", i)[0:S, :].rearrange("p (b d) -> p b d", b=2),
                                                b_f2[:, :].unsqueeze(1).to_broadcast([S, 2, D]),
                                                ALU.add).then_inc(s_tile_dve, 1)

                    def conv(m):
                        wait_freed(dve, "w_in", m)

                        def seqs(a):
                            return a.rearrange("p (b t) -> p b t", b=NB)

                        link(nc.vector.scalar_tensor_tensor(out=seqs(u[:, m]), in0=padded[:, m, :, 1:S + 1],
                                                            scalar=w_conv[:, m, 1:2], in1=seqs(u[:, m]), op0=ALU.mult,
                                                            op1=ALU.add))
                        nc.vector.scalar_tensor_tensor(out=seqs(u[:, m]), in0=padded[:, m, :, 0:S],
                                                       scalar=w_conv[:, m, 0:1], in1=seqs(u[:, m]), op0=ALU.mult,
                                                       op1=ALU.add).then_inc(s_conv, 1)

                    def delta_(i):
                        dve.wait_ge(s_log, 1)
                        wait_freed(dve, "w_dt", KI - 1)
                        if scan:
                            dve.wait_ge(s_decay, UNITS)
                        link(nc.vector.tensor_tensor(delta[:, :, :], linear, soft, ALU.add))

                    def du_(i):
                        if scan:
                            dve.wait_ge(s_term, UNITS)
                        nc.vector.tensor_tensor(du[:, :, :], delta[:, :, :], u[:, :, :], ALU.mult)

                    stages = dict(state=state, read=read, add=add, z=z, w_out=w_out_, moments_post=moments_post,
                                  norm_post=norm_post, low_post=low_post, low_gelu=low_gelu, mean_sq=mean_sq_,
                                  rms_inv=rms_inv_, down=down, qk=qk_, v=v_, maxima=maxima, normalise=normalise, f2=f2,
                                  moments_pre=moments_pre, norm_pre=norm_pre, conv=conv, delta=delta_, du=du_)
                    for name, i in plan(DVE_PLAN, scan, post, pre):
                        stages[name](i)

            nc.all_engine_barrier(sems_to_clear=clear)

        x_t = ins["x_t"]
        out_g = out.rearrange("(g b) s d -> g s b d", b=NB)
        x_g = x_t.rearrange("c (g t) -> g c t", g=GROUPS)
        step(1, False, False, True, x_g[0])
        step(0, True, False, True, x_g[1])
        with nc.Fori(0, (GROUPS - 2) // 2) as i:
            step(1, True, True, True, x_g[bass.ds(2 * i + 2, 1)], out_g[bass.ds(2 * i, 1)])
            step(0, True, True, True, x_g[bass.ds(2 * i + 3, 1)], out_g[bass.ds(2 * i + 1, 1)])
        step(1, True, True, False, None, out_g[GROUPS - 2])
        step(0, False, True, False, None, out_g[GROUPS - 1])


def positions():
    pos = np.arange(S, dtype=np.float32)[:, None]
    div = np.exp(np.arange(0, D, 2, dtype=np.float32) * np.float32(-np.log(10000.0) / D))
    ang = pos * div
    return np.stack([np.sin(ang), np.cos(ang)], axis=-1).reshape(S, D).astype(np.float32)


def tiles(a):
    return np.ascontiguousarray(a.reshape(-1, P, a.shape[-1]).transpose(1, 0, 2))


def column(a):
    return np.ascontiguousarray(a.reshape(-1, P).T)


def kernel(**inputs):
    import concourse.bacc as bacc
    from concourse.bass_utils import run_bass_kernel_spmd

    v = {k: np.asarray(a) for k, a in inputs.items()}
    tok = {k[7:]: a for k, a in v.items() if k.startswith("L0_tok_")}
    ssm = {k[8:]: a for k, a in v.items() if k.startswith("L0_attn_")}
    flat = {k: tok[k].reshape(D, D) for k in ("Wq", "Wk", "Wv")}
    cols = np.concatenate([column(tok["bp"]), column(tok["rb1_hb"]), column(tok["rb1_fb"]),
                           column(tok["bq"].reshape(-1)), column(tok["bk"].reshape(-1)), column(tok["rb2_hb"]),
                           column(tok["f2b"]), np.zeros((P, 4), np.float32)], axis=1)
    arrays = {
        "x_t": v["x"].reshape(B * S, PATCH).T,
        "ident": np.eye(P, dtype=np.float32),
        "emb": tiles(np.concatenate([tok["Wp"], positions().T], axis=1)),
        "cols": cols,
        "hw1": tiles(tok["rb1_hw"].T), "fw1": tok["rb1_fw"].T,
        "proj": tiles(np.concatenate([flat["Wq"].T, flat["Wk"].T], axis=1)), "proj_v": tiles(flat["Wv"].T),
        "rows": np.concatenate([tok["bv"].reshape(-1), tok["f2b"], tok["rb2_fb"]])[None, :],
        "hw2": tiles(tok["rb2_hw"].T), "fw2": tok["rb2_fw"].T,
        "f2_nat": tiles(tok["f2w"]), "f2_t": tiles(tok["f2w"].T),
        "up": tiles(v["L0_ffn_w_up"].T).reshape(P, -1), "down": tiles(v["L0_ffn_w_down"].T).reshape(P, -1),
        "a_log": tiles(ssm["A_log"]), "d_col": column(ssm["D_param"]),
        "f1": tiles(tok["f1w"].T), "f1b": column(tok["f1b"]),
        "w_in": tiles(ssm["W_in"]), "w_conv": tiles(ssm["W_conv"]), "w_x": tiles(ssm["W_x"]), "w_dt": ssm["W_dt"],
        "b_dt": column(ssm["b_dt"]), "w_out": tiles(ssm["W_out"]),
    }
    nc = bacc.Bacc("TRN2", target_bir_lowering=False, num_devices=1)
    feeds, aps = {}, {}
    for name, a in arrays.items():
        a = np.ascontiguousarray(a)
        feeds[f"in_{name}"] = a
        aps[name] = nc.dram_tensor(f"in_{name}", a.shape, mybir.dt.from_np(a.dtype), kind="ExternalInput").ap()
    out = nc.dram_tensor("out_0", (B, S, D), F32, kind="ExternalOutput").ap()
    build(nc, aps, out)
    r = run_bass_kernel_spmd(nc, [feeds], core_ids=[0])
    return r.results[0]["out_0"]
```

```python
from contextlib import ExitStack

import numpy as np

import concourse.bass as bass
from concourse import mybir

F32 = mybir.dt.float32
F16 = mybir.dt.float16
ALU = mybir.AluOpType
ACT = mybir.ActivationFunctionType
AX = mybir.AxisListType

P = 128
B, S, PATCH, D = 64, 125, 32, 256
HEADS, DK = 4, 64
FF = 1024
DI, NS, DT_RANK = 512, 16, 16
NB = 4
T = NB * S
GROUPS = B // NB
KD, KI, KF = D // P, DI // P, FF // P
Z = PATCH + S
LN_EPS, RMS_EPS = 1e-5, 1e-8
SLOTS = 4
UNITS = 2 * NS
HT = KI // 2
DA_SLOTS, W_SLOTS, BC_SLOTS = 3, 6, 4
POOL_PAIRS = [2, 4, 6, 8, 10, 12, 14]
VECTOR_PAIRS = [q for q in range(NS) if q not in POOL_PAIRS]

PE_PLAN = """
    qk*4 v score*2 v w_out score w_out turn_p score w_out turn_p w_out sum turn_p pv turn_p pv f1*2 turn_post*2 sum
    f1*3 sum up f1 up sum f1 up f1 up sum up*2 sum f2*2 up*2 sum f2*2 down*2 sumsq down*2 sum*3 turn_pre*2 w_in*5
    sum w_in*3 sum w_x sum w_dt*4 sum*3
"""
ACT_PLAN = """
    decay*3 softmax*2 normalise*2 softmax turn_p decay softmax normalise turn_p normalise turn_p*2 pv*2 decay
    norm_post decay f1 high decay f1 decay f1 high decay*3 f1 decay f1 gelu*2 f1*2 square gelu square*2 gelu f1
    decay*5 square gelu*2 square decay square decay gelu square gelu decay square decay*3 norm_pre turn_pre*2
    decay*2 store w_in decay w_in*2 decay*2 gate w_in silu*2 gate silu gate*2 silu decay*3 w_x decay abs*4
    soft_exp*2 soft_log*2
"""
DVE_PLAN = """
    z*2 qk*4 z*2 maxima v maxima state*2 invert read invert maxima v w_out read maxima invert add skip state w_out
    invert state moments_post read*2 shift_post add skip state*2 read*2 low_post state*2 low_post read state read
    add read state read low_gelu state read low_gelu state read add state*2 low_gelu state read*2 low_gelu state
    low_gelu read*2 state read low_gelu state read low_gelu*2 f2 add f2 state read state mean_sq read rms_inv down*2
    moments_pre add shift_pre state read state read state read state conv state conv read conv read state add read
    conv state*2 read*2 state add state read*2 state read state read add delta du
"""
POOL_PLAN = """
    term*7 root_post term*2 add term*4 add square_sum term square_sum term*3 add square_sum term square_sum*2 term
    square_sum term square_sum add rms term root_pre term*4 add term*3 add term*4 add delta du
"""
SCAN_STAGES = {"skip", "sum", "decay", "state", "read", "add", "term"}
POST_STAGES = {"z", "w_out", "turn_post", "up", "sumsq", "down", "high", "gelu", "square", "store", "moments_post",
               "shift_post", "norm_post", "low_post", "low_gelu", "mean_sq", "rms_inv", "root_post", "square_sum",
               "rms"}
FREED_BY = dict(w_out="w_out", turn_post="low_post", up="gelu", sumsq="mean_sq", down="down", qk="qk", v="v",
                score="softmax", turn_p="turn_p", pv="pv", f1="f1", f2="f2", turn_pre="turn_pre", w_x="w_x",
                w_dt="abs")
PER_TILE = dict(w_out=2, down=2, f2=2)


def plan(text, scan, post, pre):
    seen = {}
    for word in text.split():
        name, _, times = word.partition("*")
        wanted = scan if name in SCAN_STAGES else post if name in POST_STAGES else pre
        for _ in range(int(times or 1)):
            i = seen[name] = seen.get(name, -1) + 1
            if wanted:
                yield name, i


def ring_tiles(scan, post, pre):
    count, freeing = {"act": 0, "dve": 0}, {}
    for who, text in (("act", ACT_PLAN), ("dve", DVE_PLAN)):
        for name, i in plan(text, scan, post, pre):
            if name in FREED_BY.values() or who == "act" and name in ("w_in", "gate"):
                count[who] += 1
                freeing[name, i] = (who, count[who])
    tile, filled, freed, frees = {}, {}, {}, []
    for name, part in plan(PE_PLAN, scan, post, pre):
        if name == "sum":
            continue
        n = PER_TILE.get(name, 1)
        i = part // n
        if part % n == 0:
            by = FREED_BY.get(name) or ("w_in" if i < KI else "gate")
            tile[name, i] = len(frees)
            freed[name, i] = freeing[by, i - KI if by == "gate" else i]
            frees.append(freed[name, i])
        if part % n == n - 1:
            filled[name, i] = len(filled) + 1
    return tile, filled, freed, frees



def build(nc, ins, out):
    with ExitStack() as ctx:
        def sb(name, shape, dt=F32):
            return ctx.enter_context(nc.sbuf_tensor(name, shape, dt))

        sems = []

        def sem(name):
            s = ctx.enter_context(nc.semaphore(name))
            sems.append(s)
            return s

        ident = sb("ident", [P, P])
        ones = sb("ones", [P, P])
        w_qk = sb("w_qk", [PATCH, 2 * D])
        w_v = sb("w_v", [PATCH, D])
        pos_qk = sb("pos_qk", [P, 4, S])
        pos_v = sb("pos_v", [S, D])
        w_f1 = sb("w_f1", [P, KD, FF])
        b_f1 = sb("b_f1", [P, KF])
        w_f2 = sb("w_f2", [P, KF, D])
        b_f2 = sb("b_f2", [S, D])
        w_in = sb("w_in", [P, KD, 2 * DI])
        w_conv = sb("w_conv", [P, KI, 3])
        w_x = sb("w_x", [P, KI, DT_RANK + 2 * NS])
        w_dt = sb("w_dt", [DT_RANK, DI])
        b_dt = sb("b_dt", [P, KI])
        neg_a = sb("neg_a", [P, KI, NS])
        d_col = sb("d_col", [P, KI])
        w_out = sb("w_out", [P, KI, D])
        w_up = sb("w_up", [P, KD, FF], F16)
        w_down = sb("w_down", [P, KF, D], F16)
        half = sb("half", [S, 2 * NB])
        minus_half = sb("minus_half", [S, NB])

        patches = sb("patches", [PATCH, T])
        region_post = sb("region_post", [P, NB * D + KD * T])
        region_pre = sb("region_pre", [P, 2 * KD * T + NB * D + 4 * T])
        region_mlp = sb("region_mlp", [P, KF * T])
        gated = region_post[:, 0:KI * T].rearrange("p (m t) -> p m t", m=KI)
        xn_post = region_post[0:S, 0:NB * D].rearrange("p (b d) -> p b d", b=NB)
        xn_parts = region_post[:, NB * D:NB * D + KD * T].bitcast(F16).rearrange(
            "p (c k t) -> p c k t", c=2, k=KD)
        square = region_post[:, 0:2 * T].rearrange("p (i t) -> p i t", i=2)
        qk = region_pre[:, 0:2 * KD * T].rearrange("p (m t) -> p m t", m=2 * KD)
        xn_t = region_pre[:, 0:KD * T].rearrange("p (k t) -> p k t", k=KD)
        after_qk = region_pre[0:S, 2 * KD * T:2 * KD * T + NB * D + 4 * T]
        v_tok = after_qk[:, 0:NB * D].rearrange("p (b d) -> p b d", b=NB)
        probs = after_qk[:, NB * D:NB * D + 2 * T].rearrange("p (i c t) -> p i c t", i=2, c=4)
        probs_t = after_qk[:, NB * D + 2 * T:NB * D + 4 * T].rearrange("p (i c t) -> p i c t", i=2, c=4)
        relu = region_pre[:, 0:KF * T].rearrange("p (m t) -> p m t", m=KF)
        xn_pre = v_tok
        g_parts = region_mlp[:, :].bitcast(F16).rearrange("p (c m t) -> p c m t", c=2, m=KF)
        padded = region_mlp[:, 0:KI * NB * (S + 2)].rearrange("p (m b t) -> p m b t", m=KI, b=NB)
        soft = region_mlp[:, 0:KI * T].rearrange("p (m t) -> p m t", m=KI)
        linear = region_mlp[:, KI * T:2 * KI * T].rearrange("p (m t) -> p m t", m=KI)
        h1_mem = sb("h1", [P, 2, NB * D])
        h1 = h1_mem[0:S, :, :].rearrange("p c (b d) -> p c b d", b=NB)
        attn_t = h1_mem[:, :, 0:KD * T].rearrange("p c (k t) -> p c k t", k=KD)
        h2 = sb("h2", [S, NB, D])
        u = sb("u", [P, KI, T])
        gate = sb("gate", [P, 2, KI, T])
        delta = sb("delta", [P, KI, T])
        du = sb("du", [P, KI, T])
        x_dbl = sb("x_dbl", [DT_RANK + 2 * NS, T])
        bc = sb("bc", [P, BC_SLOTS, 2, T])
        decay = sb("decay", [P, DA_SLOTS, HT, T])
        work = sb("work", [P, W_SLOTS, HT, T])
        gelu = sb("gelu", [P, 2, T])
        sumsq = sb("sumsq", [P, T])
        row_max = sb("row_max", [S, 4])
        neg_max = sb("neg_max", [S, 2, 4])
        row_sum = sb("row_sum", [S, 2, 4])
        row_inv = sb("row_inv", [S, 2, 4])
        stats = sb("stats", [S, 2, NB, 6])
        mean_var = sb("mean_var", [S, 2, NB, 2])
        var_in = sb("var_in", [S, 2, NB])
        var_pre = sb("var_pre", [S, NB])
        root = sb("root", [S, 2, NB])
        denom = sb("denom", [S, NB])
        norm = sb("norm", [S, NB])
        shift = sb("shift", [S, 2, NB])
        mean_sq = sb("mean_sq", [S, NB])
        rms = sb("rms", [S, NB])
        rms_eps = sb("rms_eps", [S, NB])
        rms_inv = sb("rms_inv", [S, NB])

        y_acc = [ctx.enter_context(nc.psum_tensor(f"y_acc{m}", [P, 512], F32)) for m in range(KI)]
        ring = [ctx.enter_context(nc.psum_tensor(f"ring{m}", [P, 512], F32)) for m in range(SLOTS)]

        bc_dram = nc.dram_tensor("bc_scratch", [2, 2, NS, T], F32, kind="Internal").ap()

        s_load_fold = sem("s_load_fold")
        s_load_tern = sem("s_load_tern")
        s_load_rest = sem("s_load_rest")
        s_pe = sem("s_pe")
        s_dve = sem("s_dve")
        s_pool = sem("s_pool")
        s_act = sem("s_act")
        s_tile = sem("s_tile")
        s_tile_act = sem("s_tile_act")
        s_tile_dve = sem("s_tile_dve")
        s_link = sem("s_link")
        s_plink = sem("s_plink")
        s_x = sem("s_x")
        s_bc = [sem(f"s_bc{i}") for i in range(BC_SLOTS)]
        s_bc_out = sem("s_bc_out")
        s_out = sem("s_out")
        s_z = sem("s_z")
        s_skip = sem("s_skip")
        s_decay = sem("s_decay")
        s_term = sem("s_term")
        s_state = sem("s_state")
        s_read = sem("s_read")
        s_pair_dve = sem("s_pair_dve")
        s_pair_pool = sem("s_pair_pool")
        s_sum = sem("s_sum")
        s_var_pre = sem("s_var_pre")
        s_var_post = sem("s_var_post")
        s_root_pre = sem("s_root_pre")
        s_root_post = sem("s_root_post")
        s_shift_pre = sem("s_shift_pre")
        s_shift_post = sem("s_shift_post")
        s_row_inv = sem("s_row_inv")
        s_xn_pre = sem("s_xn_pre")
        s_xn_post = sem("s_xn_post")
        s_high = sem("s_high")
        s_low = sem("s_low")
        s_square = sem("s_square")
        s_sq = sem("s_sq")
        s_ms = sem("s_ms")
        s_rms_inv = sem("s_rms_inv")
        s_nmax = sem("s_nmax")
        s_probs = sem("s_probs")
        s_conv = sem("s_conv")
        s_u = sem("s_u")
        s_abs = sem("s_abs")
        s_log = sem("s_log")
        s_soft = sem("s_soft")
        s_delta_dve = sem("s_delta_dve")
        s_delta_pool = sem("s_delta_pool")
        s_du_dve = sem("s_du_dve")
        s_du_pool = sem("s_du_pool")
        clear = range(min(s.num for s in sems), max(s.num for s in sems) + 1)
        assert len(clear) == len(sems)

        tmp = [bc[:, :, :, :].rearrange("p a m t -> p (a m t)"), region_pre[:, :],
               gate[:, :, :, :].rearrange("p a m t -> p (a m t)")]

        def scratch(i, lo, n, parts=P):
            return tmp[i][0:parts, lo:lo + n]

        up_raw = work[:, :, :, :].rearrange("p a m t -> p (a m t)")[:, 0:KD * FF]
        down_raw = work[:, :, :, :].rearrange("p a m t -> p (a m t)")[:, 2048:2048 + KF * D]
        below = region_mlp[:, 0:2048]
        f2_nat = scratch(0, 0, KD * FF).rearrange("p (k f) -> p k f", k=KD)
        f2_t = scratch(1, 0, KF * D).rearrange("p (k f) -> p k f", k=KF)
        proj = scratch(2, 0, 1024).rearrange("p (k f) -> p k f", k=KD)
        proj_v = scratch(2, 1024, 512).rearrange("p (k f) -> p k f", k=KD)
        hw1 = scratch(2, 1536, 256).rearrange("p (k f) -> p k f", k=KD)
        fw1 = scratch(2, 1792, 256)
        hw2 = scratch(2, 2048, 256).rearrange("p (k f) -> p k f", k=KD)
        fw2 = scratch(2, 2304, 256)
        emb = scratch(2, 2560, KD * Z).rearrange("p (k z) -> p k z", k=KD)
        emb2 = scratch(2, 2900, KD * Z).rearrange("p (k z) -> p k z", k=KD)
        hid1 = scratch(2, 3240, Z)
        c1_rep = scratch(2, 3400, P)
        cols = scratch(2, 3540, 16)
        small = scratch(2, 3560, 16)
        rows = scratch(0, 2100, 768, 1)
        hid2 = region_post[:, 0:FF]

        loads_fold = [
            (ident[:, :], "ident"), (emb[:, :, :], "emb"), (cols, "cols"), (hw1, "hw1"), (fw1, "fw1"), (hw2, "hw2"),
            (fw2, "fw2"), (proj, "proj"), (proj_v, "proj_v"), (rows, "rows"), (f2_nat, "f2_nat"),
        ]
        loads_tern = [(up_raw, "up"), (down_raw, "down")]
        loads_rest = [
            (f2_t, "f2_t"), (neg_a[:, :, :], "a_log"), (d_col[:, :], "d_col"), (w_f1[:, :, :], "f1"),
            (b_f1[:, :], "f1b"), (w_in[:, :, :], "w_in"), (w_conv[:, :, :], "w_conv"), (w_x[:, :, :], "w_x"),
            (w_dt[:, :], "w_dt"), (b_dt[:, :], "b_dt"), (w_out[:, :, :], "w_out"),
        ]
        groups = [(loads_fold, s_load_fold), (loads_tern, s_load_tern), (loads_rest, s_load_rest)]
        with nc.Block() as block:
            @block.sync
            def _(sp):
                for loads, loaded in groups:
                    for dst, name in loads:
                        sp.dma_start(dst, ins[name]).then_inc(loaded, 16)
                for loads, loaded in groups:
                    sp.wait_ge(loaded, 16 * len(loads))

            @block.gpsimd
            def _(pool):
                nc.gpsimd.memset(decay[:, :, :, :], 0.0).then_inc(s_pool, 1)

            @block.scalar
            def _(act):
                act.wait_ge(s_load_rest, 16 * len(loads_rest))
                nc.scalar.activation(neg_a[:, :, :], neg_a[:, :, :], ACT.Exp).then_inc(s_act, 1)

            @block.tensor
            def _(pe):
                pe.wait_ge(s_load_fold, 16 * len(loads_fold))
                pe.wait_ge(s_dve, 2)
                for k in range(KD):
                    mm = nc.tensor.matmul(ring[0][:, 0:Z], hw1[:, k, :], emb[:, k, :], start=(k == 0),
                                          stop=(k == KD - 1))
                mm.then_inc(s_pe, 1)
                for k in range(KD):
                    for h in range(2):
                        mm = nc.tensor.matmul(ring[2 + h][:, :], hw2[:, k, :], f2_nat[:, k, h * 512:(h + 1) * 512],
                                              start=(k == 0), stop=(k == KD - 1))
                for k in range(KD):
                    mm = nc.tensor.matmul(y_acc[0][:, 0:1], hw2[:, k, :], cols[:, 10 + k:11 + k], start=(k == 0),
                                          stop=(k == KD - 1))
                mm.then_inc(s_pe, 1)
                pe.wait_ge(s_dve, 3)
                for m in range(KD):
                    mm = nc.tensor.matmul(ring[m][:, 0:Z], fw1[:, m * P:(m + 1) * P], hid1, start=True, stop=True)
                mm.then_inc(s_pe, 1)
                for i in range(2):
                    pe.wait_ge(s_dve, 4 + i)
                    mm = nc.tensor.matmul(y_acc[1 + i][:, 0:1], ones[:, :], small[:, 1 + i:2 + i], start=True,
                                          stop=True)
                mm.then_inc(s_pe, 1)
                pe.wait_ge(s_dve, 6)
                for m in range(4):
                    for k in range(KD):
                        mm = nc.tensor.matmul(ring[0][:, m * S:(m + 1) * S], proj[:, k, m * P:(m + 1) * P],
                                              emb2[:, k, PATCH:Z], start=(k == 0), stop=(k == KD - 1))
                for k in range(KD):
                    mm = nc.tensor.matmul(ring[1][0:PATCH, :], emb2[:, k, 0:PATCH], proj[:, k, :], start=(k == 0),
                                          stop=(k == KD - 1))
                mm.then_inc(s_pe, 1)
                pe.wait_ge(s_dve, 8)
                for k in range(KD):
                    mm = nc.tensor.matmul(y_acc[0][0:PATCH, 0:D], emb2[:, k, 0:PATCH], proj_v[:, k, :],
                                          start=(k == 0), stop=(k == KD - 1))
                for k in range(KD):
                    nc.tensor.matmul(y_acc[1][0:S, 0:D], emb2[:, k, PATCH:Z], proj_v[:, k, :], start=(k == 0),
                                     stop=False)
                nc.tensor.matmul(y_acc[1][0:S, 0:D], ones[0:1, 0:S], rows[0:1, 0:D], start=False, stop=True)
                nc.tensor.matmul(y_acc[2][0:S, 0:D], c1_rep[:, 0:S], fw2, start=True, stop=False)
                nc.tensor.matmul(y_acc[2][0:S, 0:D], ones[0:1, 0:S], rows[0:1, D:2 * D], start=False, stop=False)
                mm = nc.tensor.matmul(y_acc[2][0:S, 0:D], ones[0:1, 0:S], rows[0:1, 2 * D:3 * D], start=False,
                                      stop=True)
                mm.then_inc(s_pe, 1)
                for f in range(KF):
                    if f >= 2:
                        pe.wait_ge(s_dve, 8 + f - 1)
                    nc.tensor.matmul(ring[2 + f % 2][:, 0:D], hid2[:, f * P:(f + 1) * P], fw2, start=True,
                                     stop=True).then_inc(s_pe, 1)

            @block.vector
            def _(dve):
                linked = [0]

                def link(ins_):
                    linked[0] += 1
                    ins_.then_inc(s_link, 1)
                    dve.wait_ge(s_link, linked[0])

                nc.vector.memset(ones[:, :], 1.0)
                nc.vector.memset(half[:, :], 0.5)
                nc.vector.memset(minus_half[:, :], -0.5).then_inc(s_dve, 1)
                dve.wait_ge(s_load_fold, 16 * len(loads_fold))
                for k in range(KD):
                    ins_ = nc.vector.tensor_scalar(emb[:, k, PATCH:Z], emb[:, k, PATCH:Z], cols[:, k:k + 1], None,
                                                   ALU.add)
                ins_.then_inc(s_dve, 1)
                dve.wait_ge(s_pe, 1)
                nc.vector.tensor_copy(hid1[:, 0:PATCH], ring[0][:, 0:PATCH])
                nc.vector.tensor_scalar(hid1[:, PATCH:Z], ring[0][:, PATCH:Z], cols[:, 2:3], None,
                                        ALU.add).then_inc(s_dve, 1)
                dve.wait_ge(s_load_tern, 16 * len(loads_tern))
                for i, w in enumerate((up_raw, down_raw)):
                    nc.vector.tensor_reduce(small[:, 1 + i:2 + i], w, AX.X, ALU.add,
                                            apply_absolute_value=True).then_inc(s_dve, 1)
                dve.wait_ge(s_pe, 4)
                for m in range(KD):
                    link(nc.vector.tensor_tensor(emb2[:, m, :], ring[m][:, 0:Z], emb[:, m, :], ALU.add))
                    ins_ = nc.vector.tensor_scalar(emb2[:, m, PATCH:Z], emb2[:, m, PATCH:Z], cols[:, 3 + m:4 + m],
                                                   None, ALU.add)
                ins_.then_inc(s_dve, 1)
                nc.vector.tensor_copy(hid2[:, 0:512], ring[2][:, :])
                nc.vector.tensor_copy(hid2[:, 512:1024], ring[3][:, :]).then_inc(s_dve, 1)
                link(nc.vector.tensor_scalar(small[:, 0:1], y_acc[0][:, 0:1], cols[:, 9:10], None, ALU.add))
                nc.vector.tensor_scalar(c1_rep, ones[:, :], small[:, 0:1], None, ALU.mult)
                for i in range(2):
                    nc.vector.tensor_scalar(small[:, 3 + i:4 + i], y_acc[1 + i][:, 0:1], 0.5 / (D * FF), None, ALU.mult)
                    ins_ = nc.vector.tensor_scalar(small[:, 5 + i:6 + i], y_acc[1 + i][:, 0:1], -0.5 / (D * FF), None,
                                                   ALU.mult)
                ins_.then_inc(s_dve, 1)
                dve.wait_ge(s_dve, 8)
                for i, (w, dst) in enumerate(((up_raw, w_up), (down_raw, w_down))):
                    flat = dst[:, :, :].rearrange("p a b -> p (a b)")
                    link(nc.vector.tensor_scalar(below, w, small[:, 5 + i:6 + i], None, ALU.is_lt))
                    link(nc.vector.scalar_tensor_tensor(out=flat, in0=w, scalar=small[:, 3 + i:4 + i], in1=below,
                                                        op0=ALU.is_gt, op1=ALU.subtract))
                dve.wait_ge(s_load_rest, 16 * len(loads_rest))
                for f in range(KF):
                    dve.wait_ge(s_pe, 7 + f)
                    nc.vector.tensor_tensor(w_f2[:, f, :], ring[2 + f % 2][:, 0:D], f2_t[:, f, :],
                                            ALU.add).then_inc(s_dve, 1)
                for m in range(4):
                    nc.vector.tensor_scalar(pos_qk[:, m, :], ring[0][:, m * S:(m + 1) * S], cols[:, 5 + m:6 + m], None,
                                            ALU.add)
                nc.vector.tensor_copy(w_qk[:, :], ring[1][0:PATCH, :])
                nc.vector.tensor_copy(w_v[:, :], y_acc[0][0:PATCH, 0:D])
                nc.vector.tensor_copy(pos_v[:, :], y_acc[1][0:S, 0:D])
                nc.vector.tensor_copy(b_f2[:, :], y_acc[2][0:S, 0:D])
                dve.wait_ge(s_act, 1)
                link(nc.vector.tensor_scalar(neg_a[:, :, :], neg_a[:, :, :], -1.0, None, ALU.mult))
        nc.all_engine_barrier(sems_to_clear=clear)

        pair_of = [(j // 4, (j // 2) % 2, 2 * (j // 4) + j % 2) for j in range(UNITS)]

        def last_unit(n):
            return 4 * (n // 2) + 2 + n % 2

        def increments(scan, post, pre):
            _, filled, _, frees = ring_tiles(scan, post, pre)
            adds = {s_skip: scan * 2, s_decay: scan * UNITS, s_term: scan * UNITS, s_state: scan * UNITS,
                    s_read: scan * UNITS, s_pair_dve: scan * len(VECTOR_PAIRS), s_pair_pool: scan * len(POOL_PAIRS),
                    s_sum: scan * NS, s_z: post * KI, s_var_post: post, s_root_post: post, s_xn_post: post * NB,
                    s_high: post * KD, s_low: post * KF, s_square: post * KF,
                    s_sq: post * (KF - 1), s_ms: post, s_rms_inv: post, s_out: post * 16, s_x: pre * 16,
                    s_bc_out: pre * 16, s_nmax: pre * 4, s_probs: pre * 4, s_var_pre: pre, s_root_pre: pre,
                    s_xn_pre: pre * NB, s_shift_pre: pre, s_shift_post: post,
                    s_row_inv: pre * 4, s_conv: pre * KI, s_u: pre * KI, s_abs: pre * KI, s_soft: pre * 2,
                    s_log: pre * 2,
                    s_delta_dve: pre, s_delta_pool: pre, s_du_dve: pre, s_du_pool: pre,
                    s_tile: len(filled)}
            for s in s_bc:
                adds[s] = scan * 16 * (NS // BC_SLOTS)
            for who, s in (("act", s_tile_act), ("dve", s_tile_dve)):
                adds[s] = sum(1 for w, _ in frees if w == who)
            return adds

        def run_of_steps(*steps):
            rings = [ring_tiles(*s[1:4]) for s in steps]
            pasts, tiles_before = [{s: 0 for s in increments(True, True, True)}], [0]
            for nth, (_, scan, post, pre, _, _) in enumerate(steps):
                adds = increments(scan, post, pre)
                pasts.append({s: pasts[nth][s] + adds[s] for s in adds})
                tiles_before.append(tiles_before[nth] + len(rings[nth][3]))
            frees = [(who, pasts[nth][s_tile_act if who == "act" else s_tile_dve] + n)
                     for nth in range(len(steps)) for who, n in rings[nth][3]]

            def wait_freed(eng, nth, name, i):
                who, n = rings[nth][2][name, i]
                sem = s_tile_act if who == "act" else s_tile_dve
                eng.wait_ge(sem, pasts[nth][sem] + n)

            def wait_tile(eng, nth, name, i):
                eng.wait_ge(s_tile, pasts[nth][s_tile] + rings[nth][1][name, i])

            def tile_of(nth, name, i):
                return tiles_before[nth] + rings[nth][0][name, i]

            def bank(nth, name, i):
                return ring[tile_of(nth, name, i) % SLOTS]

            def wait_bank(eng, nth, name, i):
                t = tile_of(nth, name, i)
                if t >= SLOTS:
                    who, n = frees[t - SLOTS]
                    eng.wait_ge(s_tile_act if who == "act" else s_tile_dve, n)

            with nc.Block() as block:
                @block.sync
                def _(sp):
                    for nth, (c, scan, post, pre, x_cols, out_rows) in enumerate(steps):
                        past, o = pasts[nth], 1 - c
                        if nth == 0 and pre:
                            sp.dma_start(patches[:, :], x_cols).then_inc(s_x, 16)
                        if scan:
                            for n in range(NS):
                                slot = n % BC_SLOTS
                                if n >= BC_SLOTS or past[s_read]:
                                    used = last_unit(n - BC_SLOTS) + 1
                                    sp.wait_ge(s_read, past[s_read] + used)
                                    sp.wait_ge(s_term, past[s_term] + used)
                                src = bc_dram[c, :, n, :].unsqueeze(0).to_broadcast([P, 2, T])
                                sp.dma_start(bc[:, slot], src).then_inc(s_bc[slot], 16)
                        if nth + 1 < len(steps) and steps[nth + 1][3]:
                            wait_tile(sp, nth, "qk", 2 * KD - 1)
                            wait_tile(sp, nth, "v", 1)
                            sp.dma_start(patches[:, :], steps[nth + 1][4]).then_inc(s_x, 16)
                        if pre:
                            for slot in range(BC_SLOTS):
                                if past[s_bc[slot]]:
                                    sp.wait_ge(s_bc[slot], past[s_bc[slot]])
                            wait_freed(sp, nth, "w_x", 0)
                            sp.dma_start(bc_dram[o].rearrange("i n t -> (i n) t"),
                                         x_dbl[DT_RANK:DT_RANK + 2 * NS, :]).then_inc(s_bc_out, 16)
                            sp.wait_ge(s_bc_out, past[s_bc_out] + 16)
                            sp.wait_ge(s_x, past[s_x] + 16)
                        if post:
                            sp.wait_ge(s_out, past[s_out] + 16)

                @block.gpsimd
                def _(pool):
                    for nth, (c, scan, post, pre, _, _) in enumerate(steps):
                        past = pasts[nth]

                        def term(j):
                            p, h, n = pair_of[j]
                            pool.wait_ge(s_bc[n % BC_SLOTS], past[s_bc[n % BC_SLOTS]] + 16 * (n // BC_SLOTS + 1))
                            if j == 0 and past[s_du_dve]:
                                pool.wait_ge(s_du_dve, past[s_du_dve])
                            if j == HT and past[s_du_pool]:
                                pool.wait_ge(s_du_pool, past[s_du_pool])
                            if past[s_term] + j >= W_SLOTS:
                                pool.wait_ge(s_sum, past[s_sum] + (j - W_SLOTS) // 2 + 1)
                            nc.gpsimd.tensor_tensor(
                                work[:, (past[s_term] + j) % W_SLOTS], du[:, HT * h:HT * h + HT, :],
                                bc[:, n % BC_SLOTS, 0].unsqueeze(1).to_broadcast([P, HT, T]),
                                ALU.mult).then_inc(s_term, 1)

                        def add(i):
                            q = POOL_PAIRS[i]
                            pool.wait_ge(s_read, past[s_read] + 2 * q + 2)
                            first = work[:, (past[s_term] + 2 * q) % W_SLOTS]
                            nc.gpsimd.tensor_tensor(first, first, work[:, (past[s_term] + 2 * q + 1) % W_SLOTS],
                                                    ALU.add).then_inc(s_pair_pool, 1)

                        def root_post(i):
                            pool.wait_ge(s_var_post, past[s_var_post] + 1)
                            nc.gpsimd.tensor_tensor(root[:, :, :], var_in[:, :, :],
                                                    half[:, :].rearrange("p (a b) -> p a b", a=2),
                                                    ALU.pow).then_inc(s_root_post, 1)

                        def root_pre(i):
                            pool.wait_ge(s_var_pre, past[s_var_pre] + 1)
                            nc.gpsimd.tensor_tensor(norm[:, :], var_pre[:, :], minus_half[:, :],
                                                    ALU.pow).then_inc(s_root_pre, 1)

                        def square_sum(i):
                            m = i + 1
                            pool.wait_ge(s_square, past[s_square] + m + 1)
                            if m >= 2:
                                pool.wait_ge(s_sq, past[s_sq] + m - 1)
                            nc.gpsimd.tensor_tensor(sumsq[:, :], sumsq[:, :], square[:, m % 2],
                                                    ALU.add).then_inc(s_sq, 1)

                        def rms_(i):
                            wait_freed(pool, nth, "sumsq", 0)
                            nc.gpsimd.tensor_tensor(rms[:, :], mean_sq[:, :], half[:, 0:NB], ALU.pow).then_inc(s_ms, 1)

                        def delta_(i):
                            pool.wait_ge(s_log, past[s_log] + 2)
                            if scan:
                                pool.wait_ge(s_decay, past[s_decay] + UNITS)
                            nc.gpsimd.tensor_tensor(delta[:, HT:KI], linear[:, HT:KI], soft[:, HT:KI],
                                                    ALU.add).then_inc(s_delta_pool, 1)

                        def du_(i):
                            if scan:
                                pool.wait_ge(s_term, past[s_term] + UNITS)
                            pool.wait_ge(s_delta_pool, past[s_delta_pool] + 1)
                            nc.gpsimd.tensor_tensor(du[:, HT:KI], delta[:, HT:KI], u[:, HT:KI],
                                                    ALU.mult).then_inc(s_du_pool, 1)

                        stages = dict(delta=delta_, du=du_, term=term, add=add, root_post=root_post, root_pre=root_pre,
                                      square_sum=square_sum, rms=rms_)
                        for name, i in plan(POOL_PLAN, scan, post, pre):
                            stages[name](i)

                @block.scalar
                def _(act):
                    for nth, (c, scan, post, pre, x_cols, out_rows) in enumerate(steps):
                        past, o = pasts[nth], 1 - c

                        def decays(j):
                            p, h, n = pair_of[j]
                            if j == 0 and past[s_delta_dve]:
                                act.wait_ge(s_delta_dve, past[s_delta_dve])
                            if j == HT and past[s_delta_pool]:
                                act.wait_ge(s_delta_pool, past[s_delta_pool])
                            if past[s_state] + j >= DA_SLOTS:
                                act.wait_ge(s_state, past[s_state] + j - DA_SLOTS + 1)
                            for m in range(HT):
                                dst = decay[:, (past[s_state] + j) % DA_SLOTS, m]
                                dst = dst.rearrange("p (b t) -> p b t", b=NB)[:, :, 1:S]
                                src = delta[:, HT * h + m].rearrange("p (b t) -> p b t", b=NB)[:, :, 1:S]
                                ins_ = nc.scalar.activation(dst, src, ACT.Exp, scale=neg_a[:, HT * h + m, n:n + 1])
                            ins_.then_inc(s_decay, 1)

                        def norm_post(i):
                            act.wait_ge(s_shift_post, past[s_shift_post] + 1)
                            for b in range(NB):
                                nc.scalar.activation(xn_post[:, b, :], h2[:, b, :], ACT.Identity,
                                                     bias=shift[:, 1, b:b + 1], scale=denom[:, b:b + 1]).then_inc(s_xn_post, 1)

                        def norm_pre(i):
                            act.wait_ge(s_shift_pre, past[s_shift_pre] + 1)
                            for b in range(NB):
                                nc.scalar.activation(xn_pre[:, b, :], h1[:, o, b, :], ACT.Identity,
                                                     bias=shift[:, 0, b:b + 1],
                                                     scale=norm[:, b:b + 1]).then_inc(s_xn_pre, 1)

                        def high(k):
                            wait_tile(act, nth, "turn_post", k)
                            nc.scalar.activation(xn_parts[:, 0, k], bank(nth, "turn_post", k)[:, 0:T],
                                                 ACT.Copy).then_inc(s_high, 1)

                        def gelu_(m):
                            wait_tile(act, nth, "up", m)
                            if past[s_low] + m >= 2:
                                act.wait_ge(s_low, past[s_low] + m - 1)
                                act.wait_ge(s_square, past[s_square] + m - 1)
                            src = bank(nth, "up", m)[:, 0:T]
                            nc.scalar.activation(g_parts[:, 0, m], src, ACT.Gelu)
                            nc.scalar.activation(gelu[:, m % 2], src, ACT.Gelu).then_inc(s_tile_act, 1)

                        def square_(m):
                            wait_freed(act, nth, "up", m)
                            if m >= 3:
                                act.wait_ge(s_sq, past[s_sq] + m - 2)
                            dst = square[:, m % 2] if m else sumsq[:, :]
                            nc.scalar.activation(dst, gelu[:, m % 2], ACT.Square).then_inc(s_square, 1)

                        def store(i):
                            wait_freed(act, nth, "down", 1)
                            act.dma_start(out_rows, h2[:, :, :]).then_inc(s_out, 16)

                        def softmax(i):
                            wait_tile(act, nth, "score", i)
                            act.wait_ge(s_nmax, past[s_nmax] + i + 1)
                            if i >= 2:
                                wait_tile(act, nth, "turn_p", i - 2)
                                act.wait_ge(s_probs, past[s_probs] + i - 1)
                            for q in range(4):
                                ins_ = nc.scalar.activation(probs[:, i % 2, q], bank(nth, "score", i)[0:S, q * S:(q + 1) * S],
                                                            ACT.Exp, bias=neg_max[:, i % 2, q:q + 1], scale=DK ** -0.5,
                                                            accum_out=row_sum[:, i % 2, q:q + 1])
                            ins_.then_inc(s_tile_act, 1)

                        def normalise(i):
                            act.wait_ge(s_row_inv, past[s_row_inv] + i + 1)
                            wait_freed(act, nth, "score", i)
                            for q in range(4):
                                ins_ = nc.scalar.activation(probs[:, i % 2, q], probs[:, i % 2, q], ACT.Identity,
                                                            scale=row_inv[:, i % 2, q:q + 1])
                            ins_.then_inc(s_probs, 1)

                        def turn_p(i):
                            wait_tile(act, nth, "turn_p", i)
                            if i >= 2:
                                wait_tile(act, nth, "pv", i // 2 - 1)
                            nc.scalar.activation(probs_t[:, i % 2].rearrange("p c t -> p (c t)"),
                                                 bank(nth, "turn_p", i)[0:S, 0:T], ACT.Copy).then_inc(s_tile_act, 1)

                        def pv(i):
                            wait_tile(act, nth, "pv", i)
                            if post:
                                wait_freed(act, nth, "w_out", 1)
                            nc.scalar.activation(attn_t[:, o, :, 2 * S * i:2 * S * (i + 1)],
                                                 bank(nth, "pv", i)[:, 0:T].rearrange("p (k t) -> p k t", k=KD),
                                                 ACT.Copy).then_inc(s_tile_act, 1)

                        def f1(m):
                            wait_tile(act, nth, "f1", m)
                            nc.scalar.activation(relu[:, m], bank(nth, "f1", m)[:, 0:T], ACT.Relu,
                                                 bias=b_f1[:, m:m + 1]).then_inc(s_tile_act, 1)

                        def turn_pre(k):
                            wait_tile(act, nth, "turn_pre", k)
                            nc.scalar.activation(xn_t[:, k], bank(nth, "turn_pre", k)[:, 0:T],
                                                 ACT.Copy).then_inc(s_tile_act, 1)

                        def w_in_(m):
                            wait_tile(act, nth, "w_in", m)
                            nc.scalar.activation(padded[:, m, :, 2:S + 2],
                                                 bank(nth, "w_in", m)[:, 0:T].rearrange("p (b t) -> p b t", b=NB), ACT.Copy)
                            if scan and m == 0:
                                act.wait_ge(s_skip, past[s_skip] + 2)
                            nc.scalar.activation(u[:, m], bank(nth, "w_in", m)[:, 0:T], ACT.Identity,
                                                 scale=w_conv[:, m, 2:3]).then_inc(s_tile_act, 1)

                        def gate_(m):
                            wait_tile(act, nth, "w_in", KI + m)
                            if post:
                                act.wait_ge(s_z, past[s_z] + KI)
                            nc.scalar.activation(gate[:, o, m], bank(nth, "w_in", KI + m)[:, 0:T],
                                                 ACT.Silu).then_inc(s_tile_act, 1)

                        def silu(m):
                            act.wait_ge(s_conv, past[s_conv] + m + 1)
                            nc.scalar.activation(u[:, m], u[:, m], ACT.Silu).then_inc(s_u, 1)

                        def w_x_(i):
                            wait_tile(act, nth, "w_x", 0)
                            if past[s_bc_out]:
                                act.wait_ge(s_bc_out, past[s_bc_out])
                            nc.scalar.activation(x_dbl[:, :], bank(nth, "w_x", 0)[0:DT_RANK + 2 * NS, 0:T],
                                                 ACT.Copy).then_inc(s_tile_act, 1)

                        def absolute(m):
                            wait_tile(act, nth, "w_dt", m)
                            act.wait_ge(s_conv, past[s_conv] + KI)
                            nc.scalar.activation(soft[:, m], bank(nth, "w_dt", m)[:, 0:T], ACT.Abs,
                                                 bias=b_dt[:, m:m + 1]).then_inc(s_abs, 1)
                            nc.scalar.activation(linear[:, m], bank(nth, "w_dt", m)[:, 0:T], ACT.Relu,
                                                 bias=b_dt[:, m:m + 1]).then_inc(s_tile_act, 1)

                        def soft_exp(h):
                            act.wait_ge(s_abs, past[s_abs] + HT * (h + 1))
                            part = soft[:, HT * h:HT * (h + 1)]
                            nc.scalar.activation(part, part, ACT.Exp, scale=-1.0).then_inc(s_soft, 1)

                        def soft_log(h):
                            act.wait_ge(s_soft, past[s_soft] + h + 1)
                            part = soft[:, HT * h:HT * (h + 1)]
                            nc.scalar.activation(part, part, ACT.Ln, bias=1.0).then_inc(s_log, 1)

                        stages = dict(decay=decays, high=high, gelu=gelu_, square=square_, store=store, softmax=softmax,
                                      normalise=normalise, norm_post=norm_post, norm_pre=norm_pre,
                                      turn_p=turn_p, pv=pv, f1=f1, turn_pre=turn_pre, w_in=w_in_, gate=gate_, silu=silu,
                                      w_x=w_x_, abs=absolute, soft_exp=soft_exp, soft_log=soft_log)
                        for name, i in plan(ACT_PLAN, scan, post, pre):
                            stages[name](i)

                @block.tensor
                def _(pe):
                    for nth, (c, scan, post, pre, _, _) in enumerate(steps):
                        past, o = pasts[nth], 1 - c

                        def sum_pair(q):
                            if q in POOL_PAIRS:
                                pe.wait_ge(s_pair_pool, past[s_pair_pool] + POOL_PAIRS.index(q) + 1)
                            elif q >= 2:
                                pe.wait_ge(s_pair_dve, past[s_pair_dve] + VECTOR_PAIRS.index(q) + 1)
                            else:
                                pe.wait_ge(s_skip, past[s_skip] + q + 1)
                                if post:
                                    pe.wait_ge(s_z, past[s_z] + HT * (q + 1))
                            for m in range(HT):
                                ins_ = nc.tensor.matmul(y_acc[HT * (q % 2) + m][:, 0:T], ident[:, :],
                                                        work[:, (past[s_term] + 2 * q) % W_SLOTS, m], start=(q < 2),
                                                        stop=(q >= NS - 2),
                                                        skip_group_check=True)
                            ins_.then_inc(s_sum, 1)

                        def w_out_(i):
                            if i == 0:
                                pe.wait_ge(s_z, past[s_z] + KI)
                            if i % 2 == 0:
                                wait_bank(pe, nth, "w_out", i // 2)
                            for k in range(KI):
                                mm = nc.tensor.matmul(bank(nth, "w_out", i // 2)[0:S, (i % 2) * D:(i % 2 + 1) * D],
                                                      gated[:, k, i * S:(i + 1) * S], w_out[:, k, :], start=(k == 0),
                                                      stop=(k == KI - 1))
                            if i % 2:
                                mm.then_inc(s_tile, 1)

                        def turn(name, k, xn):
                            wait_bank(pe, nth, name, k)
                            for b in range(NB):
                                mm = nc.tensor.transpose(bank(nth, name, k)[:, b * S:(b + 1) * S],
                                                         xn[:, b, k * P:(k + 1) * P], ident[0:S, 0:S])
                            mm.then_inc(s_tile, 1)

                        def turn_post(k):
                            pe.wait_ge(s_xn_post, past[s_xn_post] + NB)
                            turn("turn_post", k, xn_post)

                        def turn_pre(k):
                            pe.wait_ge(s_xn_pre, past[s_xn_pre] + NB)
                            turn("turn_pre", k, xn_pre)

                        def up(m):
                            wait_freed(pe, nth, "turn_post", 1)
                            wait_bank(pe, nth, "up", m)
                            for k in range(KD):
                                for part in range(2):
                                    mm = nc.tensor.matmul(bank(nth, "up", m)[:, 0:T], w_up[:, k, m * P:(m + 1) * P],
                                                          xn_parts[:, part, k], start=(k == 0 and part == 0),
                                                          stop=(k == KD - 1 and part == 1))
                            mm.then_inc(s_tile, 1)

                        def sumsq_(i):
                            pe.wait_ge(s_sq, past[s_sq] + KF - 1)
                            wait_bank(pe, nth, "sumsq", 0)
                            for b in range(NB):
                                mm = nc.tensor.matmul(bank(nth, "sumsq", 0)[0:S, b:b + 1], sumsq[:, b * S:(b + 1) * S],
                                                      ones[:, 0:1], start=True, stop=True)
                            mm.then_inc(s_tile, 1)

                        def down(i):
                            if i == 0:
                                pe.wait_ge(s_low, past[s_low] + KF)
                            if i % 2 == 0:
                                wait_bank(pe, nth, "down", i // 2)
                            for m in range(KF):
                                for part in range(2):
                                    mm = nc.tensor.matmul(bank(nth, "down", i // 2)[0:S, (i % 2) * D:(i % 2 + 1) * D],
                                                          g_parts[:, part, m, i * S:(i + 1) * S], w_down[:, m, :],
                                                          start=(m == 0 and part == 0),
                                                          stop=(m == KF - 1 and part == 1))
                            if i % 2:
                                mm.then_inc(s_tile, 1)

                        def qk_(m):
                            pe.wait_ge(s_x, past[s_x] + 16)
                            wait_bank(pe, nth, "qk", m)
                            nc.tensor.matmul(bank(nth, "qk", m)[:, 0:T], w_qk[:, m * P:(m + 1) * P], patches[:, :], start=True,
                                             stop=True).then_inc(s_tile, 1)

                        def v_(i):
                            pe.wait_ge(s_x, past[s_x] + 16)
                            wait_bank(pe, nth, "v", i)
                            for b in range(2):
                                t0 = (2 * i + b) * S
                                mm = nc.tensor.matmul(bank(nth, "v", i)[0:S, b * D:(b + 1) * D], patches[:, t0:t0 + S],
                                                      w_v[:, :], start=True, stop=True)
                            mm.then_inc(s_tile, 1)

                        def score(i):
                            wait_freed(pe, nth, "qk", 2 * KD - 1)
                            wait_bank(pe, nth, "score", i)
                            r = DK * (i % 2)
                            for hh in range(2):
                                for b in range(2):
                                    t0 = (2 * (i // 2) + b) * S
                                    q = 2 * hh + b
                                    mm = nc.tensor.matmul(bank(nth, "score", i)[0:S, q * S:(q + 1) * S],
                                                          qk[r:r + DK, hh, t0:t0 + S], qk[r:r + DK, 2 + hh, t0:t0 + S],
                                                          start=True, stop=True)
                            mm.then_inc(s_tile, 1)

                        def turn_p(i):
                            pe.wait_ge(s_probs, past[s_probs] + i + 1)
                            wait_bank(pe, nth, "turn_p", i)
                            for q in range(4):
                                mm = nc.tensor.transpose(bank(nth, "turn_p", i)[0:S, q * S:(q + 1) * S], probs[:, i % 2, q],
                                                         ident[0:S, 0:S])
                            mm.then_inc(s_tile, 1)

                        def pv(i):
                            wait_freed(pe, nth, "turn_p", 2 * i + 1)
                            wait_freed(pe, nth, "v", 1)
                            wait_bank(pe, nth, "pv", i)
                            for odd in range(2):
                                for hh in range(2):
                                    for b in range(2):
                                        q = 2 * hh + b
                                        h0 = (2 * hh + odd) * DK
                                        mm = nc.tensor.matmul(bank(nth, "pv", i)[DK * odd:DK * (odd + 1), q * S:(q + 1) * S],
                                                              v_tok[:, 2 * i + b, h0:h0 + DK], probs_t[:, odd, q],
                                                              start=True, stop=True)
                            mm.then_inc(s_tile, 1)

                        def f1(m):
                            wait_freed(pe, nth, "pv", 1)
                            wait_bank(pe, nth, "f1", m)
                            for k in range(KD):
                                mm = nc.tensor.matmul(bank(nth, "f1", m)[:, 0:T], w_f1[:, k, m * P:(m + 1) * P], attn_t[:, o, k],
                                                      start=(k == 0), stop=(k == KD - 1))
                            mm.then_inc(s_tile, 1)

                        def f2(i):
                            if i == 0:
                                wait_freed(pe, nth, "f1", KF - 1)
                            if i % 2 == 0:
                                wait_bank(pe, nth, "f2", i // 2)
                            for m in range(KF):
                                mm = nc.tensor.matmul(bank(nth, "f2", i // 2)[0:S, (i % 2) * D:(i % 2 + 1) * D],
                                                      relu[:, m, i * S:(i + 1) * S], w_f2[:, m, :], start=(m == 0),
                                                      stop=(m == KF - 1))
                            if i % 2:
                                mm.then_inc(s_tile, 1)

                        def w_in_(m):
                            wait_freed(pe, nth, "turn_pre", 1)
                            wait_bank(pe, nth, "w_in", m)
                            for k in range(KD):
                                mm = nc.tensor.matmul(bank(nth, "w_in", m)[:, 0:T], w_in[:, k, m * P:(m + 1) * P], xn_t[:, k],
                                                      start=(k == 0), stop=(k == KD - 1))
                            mm.then_inc(s_tile, 1)

                        def w_x_(i):
                            pe.wait_ge(s_u, past[s_u] + KI)
                            wait_bank(pe, nth, "w_x", 0)
                            for k in range(KI):
                                mm = nc.tensor.matmul(bank(nth, "w_x", 0)[0:DT_RANK + 2 * NS, 0:T], w_x[:, k, :], u[:, k],
                                                      start=(k == 0), stop=(k == KI - 1))
                            mm.then_inc(s_tile, 1)

                        def w_dt_(m):
                            wait_freed(pe, nth, "w_x", 0)
                            wait_bank(pe, nth, "w_dt", m)
                            nc.tensor.matmul(bank(nth, "w_dt", m)[:, 0:T], w_dt[:, m * P:(m + 1) * P], x_dbl[0:DT_RANK, :],
                                             start=True, stop=True).then_inc(s_tile, 1)

                        stages = dict(sum=sum_pair, w_out=w_out_, turn_post=turn_post, up=up, sumsq=sumsq_,
                                      down=down, qk=qk_, v=v_, score=score, turn_p=turn_p, pv=pv, f1=f1, f2=f2,
                                      turn_pre=turn_pre, w_in=w_in_, w_x=w_x_, w_dt=w_dt_)
                        for name, i in plan(PE_PLAN, scan, post, pre):
                            stages[name](i)

                @block.vector
                def _(dve):
                    linked = [0]

                    def link(ins_):
                        linked[0] += 1
                        ins_.then_inc(s_link, 1)
                        dve.wait_ge(s_link, linked[0])

                    for nth, (c, scan, post, pre, _, _) in enumerate(steps):
                        past, o = pasts[nth], 1 - c

                        def state(j):
                            dve.wait_ge(s_decay, past[s_decay] + j + 1)
                            dve.wait_ge(s_term, past[s_term] + j + 1)
                            w = work[:, (past[s_term] + j) % W_SLOTS].rearrange("p m t -> p (m t)")
                            a = decay[:, (past[s_state] + j) % DA_SLOTS].rearrange("p m t -> p (m t)")
                            nc.vector.tensor_tensor_scan(w, a, w, 0.0, ALU.mult, ALU.add).then_inc(s_state, 1)

                        def read(j):
                            p, h, n = pair_of[j]
                            dve.wait_ge(s_state, past[s_state] + j + 1)
                            w = work[:, (past[s_term] + j) % W_SLOTS]
                            nc.vector.tensor_tensor(w, w, bc[:, n % BC_SLOTS, 1].unsqueeze(1).to_broadcast([P, HT, T]),
                                                    ALU.mult).then_inc(s_read, 1)

                        def add(i):
                            q = VECTOR_PAIRS[i]
                            dve.wait_ge(s_read, past[s_read] + 2 * q + 2)
                            first = work[:, (past[s_term] + 2 * q) % W_SLOTS]
                            nc.vector.tensor_tensor(first, first, work[:, (past[s_term] + 2 * q + 1) % W_SLOTS],
                                                    ALU.add).then_inc(s_pair_dve, 1)

                        def skip(q):
                            dve.wait_ge(s_pair_dve, past[s_pair_dve] + q + 1)
                            for m in range(HT):
                                y = work[:, (past[s_term] + 2 * q) % W_SLOTS, m]
                                ins_ = nc.vector.scalar_tensor_tensor(out=y, in0=u[:, HT * q + m],
                                                                      scalar=d_col[:, HT * q + m:HT * q + m + 1], in1=y,
                                                                      op0=ALU.mult, op1=ALU.add)
                            ins_.then_inc(s_skip, 1)

                        def z(m):
                            if past[s_sum]:
                                dve.wait_ge(s_sum, past[s_sum])
                            nc.vector.tensor_tensor(gated[:, m], y_acc[m][:, 0:T], gate[:, o, m],
                                                    ALU.mult).then_inc(s_z, 1)

                        def w_out_(i):
                            wait_tile(dve, nth, "w_out", i)
                            if past[s_out]:
                                dve.wait_ge(s_out, past[s_out])
                            nc.vector.tensor_tensor(h2[:, 2 * i:2 * i + 2, :],
                                                    bank(nth, "w_out", i)[0:S, :].rearrange("p (b d) -> p b d", b=2),
                                                    h1[:, o, 2 * i:2 * i + 2, :], ALU.add).then_inc(s_tile_dve, 1)

                        def moments(h, i):
                            for b in range(NB):
                                ins_ = nc.vector.bn_stats(stats[:, i, b, :], h[:, b, :])
                            link(ins_)
                            for b in range(NB):
                                ins_ = nc.vector.bn_aggr(mean_var[:, i, b, :], stats[:, i, b, :])
                            link(ins_)

                        def moments_post(i):
                            wait_freed(dve, nth, "w_out", 1)
                            moments(h2, 1)
                            nc.vector.tensor_copy(var_in[:, 0, :], mean_var[:, 1, :, 1])
                            nc.vector.tensor_scalar(var_in[:, 1, :], mean_var[:, 1, :, 1], LN_EPS, None,
                                                    ALU.add).then_inc(s_var_post, 1)

                        def shift_post(i):
                            dve.wait_ge(s_root_post, past[s_root_post] + 1)
                            link(nc.vector.scalar_tensor_tensor(out=denom[:, :], in0=root[:, 1, :], scalar=RMS_EPS,
                                                                in1=root[:, 0, :], op0=ALU.mult, op1=ALU.add))
                            link(nc.vector.reciprocal(denom[:, :], denom[:, :]))
                            nc.vector.scalar_tensor_tensor(out=shift[:, 1, :], in0=mean_var[:, 1, :, 0], scalar=-1.0,
                                                           in1=denom[:, :], op0=ALU.mult,
                                                           op1=ALU.mult).then_inc(s_shift_post, 1)

                        def moments_pre(i):
                            wait_freed(dve, nth, "f2", 1)
                            moments(h1[:, o], 0)
                            nc.vector.tensor_scalar(var_pre[:, :], mean_var[:, 0, :, 1], LN_EPS, None,
                                                    ALU.add).then_inc(s_var_pre, 1)
                            if post:
                                wait_tile(dve, nth, "down", 1)
                            nc.vector.memset(padded[:, :, :, 0:2], 0.0)

                        def shift_pre(i):
                            dve.wait_ge(s_root_pre, past[s_root_pre] + 1)
                            nc.vector.scalar_tensor_tensor(out=shift[:, 0, :], in0=mean_var[:, 0, :, 0], scalar=-1.0,
                                                           in1=norm[:, :], op0=ALU.mult,
                                                           op1=ALU.mult).then_inc(s_shift_pre, 1)

                        def low_post(k):
                            dve.wait_ge(s_high, past[s_high] + k + 1)
                            nc.vector.tensor_tensor(xn_parts[:, 1, k], bank(nth, "turn_post", k)[:, 0:T], xn_parts[:, 0, k],
                                                    ALU.subtract).then_inc(s_tile_dve, 1)

                        def low_gelu(m):
                            wait_freed(dve, nth, "up", m)
                            nc.vector.tensor_tensor(g_parts[:, 1, m], gelu[:, m % 2], g_parts[:, 0, m],
                                                    ALU.subtract).then_inc(s_low, 1)

                        def mean_sq_(i):
                            wait_tile(dve, nth, "sumsq", 0)
                            nc.vector.tensor_scalar(mean_sq[:, :], bank(nth, "sumsq", 0)[0:S, 0:NB], 1.0 / FF, None,
                                                    ALU.mult).then_inc(s_tile_dve, 1)

                        def rms_inv_(i):
                            dve.wait_ge(s_ms, past[s_ms] + 1)
                            link(nc.vector.tensor_scalar(rms_eps[:, :], rms[:, :], RMS_EPS, None, ALU.add))
                            nc.vector.reciprocal(rms_inv[:, :], rms_eps[:, :]).then_inc(s_rms_inv, 1)

                        def down(i):
                            dve.wait_ge(s_rms_inv, past[s_rms_inv] + 1)
                            wait_tile(dve, nth, "down", i)
                            for b in range(2):
                                s = 2 * i + b
                                ins_ = nc.vector.scalar_tensor_tensor(
                                    out=h2[:, s, :], in0=bank(nth, "down", i)[0:S, b * D:(b + 1) * D],
                                    scalar=rms_inv[:, s:s + 1], in1=h2[:, s, :], op0=ALU.mult, op1=ALU.add)
                            ins_.then_inc(s_tile_dve, 1)

                        def qk_(m):
                            wait_tile(dve, nth, "qk", m)
                            nc.vector.tensor_tensor(
                                qk[:, m].rearrange("p (b t) -> p b t", b=NB),
                                bank(nth, "qk", m)[:, 0:T].rearrange("p (b t) -> p b t", b=NB),
                                pos_qk[:, m].unsqueeze(1).to_broadcast([P, NB, S]), ALU.add).then_inc(s_tile_dve, 1)

                        def v_(i):
                            wait_tile(dve, nth, "v", i)
                            nc.vector.tensor_tensor(
                                v_tok[:, 2 * i:2 * i + 2, :], bank(nth, "v", i)[0:S, :].rearrange("p (b d) -> p b d", b=2),
                                pos_v[:, :].unsqueeze(1).to_broadcast([S, 2, D]), ALU.add).then_inc(s_tile_dve, 1)

                        def maxima(i):
                            wait_tile(dve, nth, "score", i)
                            if i >= 2:
                                wait_freed(dve, nth, "score", i - 2)
                            if past[s_nmax] + i >= 1:
                                dve.wait_ge(s_nmax, past[s_nmax] + i)
                            link(nc.vector.tensor_reduce(row_max[:, :],
                                                         bank(nth, "score", i)[0:S, 0:T].rearrange("p (q t) -> p q t", q=4),
                                                         AX.X, ALU.max))
                            nc.vector.tensor_scalar(neg_max[:, i % 2, :], row_max[:, :], -DK ** -0.5, None,
                                                    ALU.mult).then_inc(s_nmax, 1)

                        def invert(i):
                            wait_freed(dve, nth, "score", i)
                            if past[s_probs] + i >= 2:
                                dve.wait_ge(s_probs, past[s_probs] + i - 1)
                            nc.vector.reciprocal(row_inv[:, i % 2, :], row_sum[:, i % 2, :]).then_inc(s_row_inv, 1)

                        def f2(i):
                            wait_tile(dve, nth, "f2", i)
                            nc.vector.tensor_tensor(h1[:, o, 2 * i:2 * i + 2, :],
                                                    bank(nth, "f2", i)[0:S, :].rearrange("p (b d) -> p b d", b=2),
                                                    b_f2[:, :].unsqueeze(1).to_broadcast([S, 2, D]),
                                                    ALU.add).then_inc(s_tile_dve, 1)

                        def conv(m):
                            wait_freed(dve, nth, "w_in", m)

                            def seqs(a):
                                return a.rearrange("p (b t) -> p b t", b=NB)

                            link(nc.vector.scalar_tensor_tensor(out=seqs(u[:, m]), in0=padded[:, m, :, 1:S + 1],
                                                                scalar=w_conv[:, m, 1:2], in1=seqs(u[:, m]), op0=ALU.mult,
                                                                op1=ALU.add))
                            nc.vector.scalar_tensor_tensor(out=seqs(u[:, m]), in0=padded[:, m, :, 0:S],
                                                           scalar=w_conv[:, m, 0:1], in1=seqs(u[:, m]), op0=ALU.mult,
                                                           op1=ALU.add).then_inc(s_conv, 1)

                        def delta_(i):
                            dve.wait_ge(s_log, past[s_log] + 1)
                            if scan:
                                dve.wait_ge(s_decay, past[s_decay] + UNITS)
                            nc.vector.tensor_tensor(delta[:, 0:HT], linear[:, 0:HT], soft[:, 0:HT],
                                                    ALU.add).then_inc(s_delta_dve, 1)

                        def du_(i):
                            if scan:
                                dve.wait_ge(s_term, past[s_term] + UNITS)
                            dve.wait_ge(s_delta_dve, past[s_delta_dve] + 1)
                            nc.vector.tensor_tensor(du[:, 0:HT], delta[:, 0:HT], u[:, 0:HT],
                                                    ALU.mult).then_inc(s_du_dve, 1)

                        stages = dict(state=state, read=read, add=add, skip=skip, z=z, w_out=w_out_,
                                      moments_post=moments_post,
                                      shift_post=shift_post, low_post=low_post, low_gelu=low_gelu, mean_sq=mean_sq_,
                                      rms_inv=rms_inv_, down=down, qk=qk_, v=v_, maxima=maxima, invert=invert, f2=f2,
                                      moments_pre=moments_pre, shift_pre=shift_pre, conv=conv, delta=delta_, du=du_)
                        for name, i in plan(DVE_PLAN, scan, post, pre):
                            stages[name](i)

            nc.all_engine_barrier(sems_to_clear=clear)

        x_t = ins["x_t"]
        out_g = out.rearrange("(g b) s d -> g s b d", b=NB)
        x_g = x_t.rearrange("c (g t) -> g c t", g=GROUPS)
        run_of_steps((1, False, False, True, x_g[0], None), (0, True, False, True, x_g[1], None))

        with nc.Fori(0, (GROUPS - 4) // 4) as i:
            run_of_steps(*[(n % 2, True, True, True, x_g[bass.ds(4 * i + (n + 1), 1)],
                            out_g[bass.ds(4 * i + (n - 1), 1)]) for n in range(1, 5)])
        run_of_steps((1, True, True, True, x_g[GROUPS - 2], out_g[GROUPS - 4]),
                     (0, True, True, True, x_g[GROUPS - 1], out_g[GROUPS - 3]),
                     (1, True, True, False, None, out_g[GROUPS - 2]), (0, False, True, False, None, out_g[GROUPS - 1]))


def positions():
    pos = np.arange(S, dtype=np.float32)[:, None]
    div = np.exp(np.arange(0, D, 2, dtype=np.float32) * np.float32(-np.log(10000.0) / D))
    ang = pos * div
    return np.stack([np.sin(ang), np.cos(ang)], axis=-1).reshape(S, D).astype(np.float32)


def tiles(a):
    return np.ascontiguousarray(a.reshape(-1, P, a.shape[-1]).transpose(1, 0, 2))


def column(a):
    return np.ascontiguousarray(a.reshape(-1, P).T)


def kernel(**inputs):
    import concourse.bacc as bacc
    from concourse.bass_utils import run_bass_kernel_spmd

    v = {k: np.asarray(a) for k, a in inputs.items()}
    tok = {k[7:]: a for k, a in v.items() if k.startswith("L0_tok_")}
    ssm = {k[8:]: a for k, a in v.items() if k.startswith("L0_attn_")}
    flat = {k: tok[k].reshape(D, D) for k in ("Wq", "Wk", "Wv")}
    cols = np.concatenate([column(tok["bp"]), column(tok["rb1_hb"]), column(tok["rb1_fb"]),
                           column(tok["bq"].reshape(-1)), column(tok["bk"].reshape(-1)), column(tok["rb2_hb"]),
                           column(tok["f2b"]), np.zeros((P, 4), np.float32)], axis=1)
    arrays = {
        "x_t": v["x"].reshape(B * S, PATCH).T,
        "ident": np.eye(P, dtype=np.float32),
        "emb": tiles(np.concatenate([tok["Wp"], positions().T], axis=1)),
        "cols": cols,
        "hw1": tiles(tok["rb1_hw"].T), "fw1": tok["rb1_fw"].T,
        "proj": tiles(np.concatenate([flat["Wq"].T, flat["Wk"].T], axis=1)), "proj_v": tiles(flat["Wv"].T),
        "rows": np.concatenate([tok["bv"].reshape(-1), tok["f2b"], tok["rb2_fb"]])[None, :],
        "hw2": tiles(tok["rb2_hw"].T), "fw2": tok["rb2_fw"].T,
        "f2_nat": tiles(tok["f2w"]), "f2_t": tiles(tok["f2w"].T),
        "up": tiles(v["L0_ffn_w_up"].T).reshape(P, -1), "down": tiles(v["L0_ffn_w_down"].T).reshape(P, -1),
        "a_log": tiles(ssm["A_log"]), "d_col": column(ssm["D_param"]),
        "f1": tiles(tok["f1w"].T), "f1b": column(tok["f1b"]),
        "w_in": tiles(ssm["W_in"]), "w_conv": tiles(ssm["W_conv"]), "w_x": tiles(ssm["W_x"]), "w_dt": ssm["W_dt"],
        "b_dt": column(ssm["b_dt"]), "w_out": tiles(ssm["W_out"]),
    }
    nc = bacc.Bacc("TRN2", target_bir_lowering=False, num_devices=1)
    feeds, aps = {}, {}
    for name, a in arrays.items():
        a = np.ascontiguousarray(a)
        feeds[f"in_{name}"] = a
        aps[name] = nc.dram_tensor(f"in_{name}", a.shape, mybir.dt.from_np(a.dtype), kind="ExternalInput").ap()
    out = nc.dram_tensor("out_0", (B, S, D), F32, kind="ExternalOutput").ap()
    build(nc, aps, out)
    r = run_bass_kernel_spmd(nc, [feeds], core_ids=[0])
    return r.results[0]["out_0"]
```
